# Optimizing a Trainium2 kernel written in Bass

```python
import numpy as np
import jax
import jax.numpy as jnp

def _softmax(x, axis=-1):
    return jax.nn.softmax(x, axis=axis)

def _gelu(x):
    return jax.nn.gelu(x, approximate=True)

def _silu(x):
    return jax.nn.silu(x)

def _sigmoid(x):
    return jax.nn.sigmoid(x)

def _layernorm(x, axis=-1, eps=1e-05):
    m = jnp.mean(x, axis=axis, keepdims=True)
    v = jnp.var(x, axis=axis, keepdims=True)
    return (x - m) / jnp.sqrt(v + eps)

def _scatter_add(tgt, idx, src, axis=0):
    return tgt.at[idx].add(src)

def _segment_sum(src, seg, n):
    return jax.ops.segment_sum(src, seg, n)
kernel_name = 'mk_metaformer_d1_conv_nchw256_r4_eb007f'

def setup_inputs(seed: int=0):
    np.random.seed(seed)
    _w = jnp.asarray

    def _rec_inputs():
        import jax
        import jax.numpy as jnp
        _gk = jax.random.key(seed)
        x = -0.0005207 + 1.001 * jax.random.normal(jax.random.fold_in(_gk, 1), (2, 64, 16, 16), jnp.float32)
        return x
    x = _rec_inputs()

    def _L0_conv_setup():
        import jax, jax.numpy as jnp
        import numpy as np
        NUM_HEADS = 8
        AREA = 4
        EPS = 1e-05

        def _conv1x1(x, w):
            return jnp.einsum('bchw,oc->bohw', x, w)

        def _bn(y, g, b, m, v):
            s = g / jnp.sqrt(v + EPS)
            return y * s[None, :, None, None] + (b - m * s)[None, :, None, None]
        key = jax.random.key(seed)
        ks = jax.random.split(key, 16)
        B, C, H, W = (2, 64, 16, 16)
        d = {}
        d['x'] = jax.random.normal(ks[0], (B, C, H, W), jnp.float32)
        d['w_qk'] = jax.random.normal(ks[1], (2 * C, C), jnp.float32) * 0.06
        d['g_qk'] = jax.random.uniform(ks[2], (2 * C,), jnp.float32, 0.5, 1.5)
        d['b_qk'] = jax.random.normal(ks[3], (2 * C,), jnp.float32) * 0.1
        d['m_qk'] = jax.random.normal(ks[4], (2 * C,), jnp.float32) * 0.1
        d['v_qk'] = jax.random.uniform(ks[5], (2 * C,), jnp.float32, 0.5, 1.5)
        d['w_v'] = jax.random.normal(ks[6], (C, C), jnp.float32) * 0.06
        d['g_v'] = jax.random.uniform(ks[7], (C,), jnp.float32, 0.5, 1.5)
        d['b_v'] = jax.random.normal(ks[8], (C,), jnp.float32) * 0.1
        d['m_v'] = jax.random.normal(ks[9], (C,), jnp.float32) * 0.1
        d['v_v'] = jax.random.uniform(ks[10], (C,), jnp.float32, 0.5, 1.5)
        d['w_p'] = jax.random.normal(ks[11], (C, C), jnp.float32) * 0.06
        d['g_p'] = jax.random.uniform(ks[12], (C,), jnp.float32, 0.5, 1.5)
        d['b_p'] = jax.random.normal(ks[13], (C,), jnp.float32) * 0.1
        d['m_p'] = jax.random.normal(ks[14], (C,), jnp.float32) * 0.1
        d['v_p'] = jax.random.uniform(ks[15], (C,), jnp.float32, 0.5, 1.5)
        return d
    _L0_conv_all = _L0_conv_setup()
    _L0_conv_in = {k: v for k, v in _L0_conv_all.items() if k in ('w_qk', 'g_qk', 'b_qk', 'm_qk', 'v_qk', 'w_v', 'g_v', 'b_v', 'm_v', 'v_v', 'w_p', 'g_p', 'b_p', 'm_p', 'v_p')}
    del _L0_conv_all

    def _L0_ffn_setup():
        import jax, jax.numpy as jnp
        import numpy as np
        TOP_K = 2
        LN_EPS = 1e-05
        key = jax.random.key(seed)
        ks = jax.random.split(key, 8)
        B, S, D, E, H = (16, 256, 64, 8, 256)
        x = jax.random.normal(ks[0], (B, S, D), dtype=jnp.float32)
        Wr = jax.random.normal(ks[1], (D, E), dtype=jnp.float32) * 0.1
        br = jnp.zeros((E,), dtype=jnp.float32)
        ln_g = jnp.ones((E, D), dtype=jnp.float32)
        ln_b = jnp.zeros((E, D), dtype=jnp.float32)
        W1 = jax.random.normal(ks[2], (E, D, H), dtype=jnp.float32) * (1.0 / np.sqrt(D))
        b1 = jnp.zeros((E, H), dtype=jnp.float32)
        W2 = jax.random.normal(ks[3], (E, H, D), dtype=jnp.float32) * (1.0 / np.sqrt(H))
        b2 = jnp.zeros((E, D), dtype=jnp.float32)
        return {'x': x, 'Wr': Wr, 'br': br, 'ln_g': ln_g, 'ln_b': ln_b, 'W1': W1, 'b1': b1, 'W2': W2, 'b2': b2}
    _L0_ffn_all = _L0_ffn_setup()
    _L0_ffn_in = {k: v for k, v in _L0_ffn_all.items() if k in ('Wr', 'br', 'ln_g', 'ln_b', 'W1', 'b1', 'W2', 'b2')}
    del _L0_ffn_all
    return {'x': x, 'L0_conv_w_qk': _L0_conv_in['w_qk'], 'L0_conv_g_qk': _L0_conv_in['g_qk'], 'L0_conv_b_qk': _L0_conv_in['b_qk'], 'L0_conv_m_qk': _L0_conv_in['m_qk'], 'L0_conv_v_qk': _L0_conv_in['v_qk'], 'L0_conv_w_v': _L0_conv_in['w_v'], 'L0_conv_g_v': _L0_conv_in['g_v'], 'L0_conv_b_v': _L0_conv_in['b_v'], 'L0_conv_m_v': _L0_conv_in['m_v'], 'L0_conv_v_v': _L0_conv_in['v_v'], 'L0_conv_w_p': _L0_conv_in['w_p'], 'L0_conv_g_p': _L0_conv_in['g_p'], 'L0_conv_b_p': _L0_conv_in['b_p'], 'L0_conv_m_p': _L0_conv_in['m_p'], 'L0_conv_v_p': _L0_conv_in['v_p'], 'L0_ffn_Wr': _L0_ffn_in['Wr'], 'L0_ffn_br': _L0_ffn_in['br'], 'L0_ffn_ln_g': _L0_ffn_in['ln_g'], 'L0_ffn_ln_b': _L0_ffn_in['ln_b'], 'L0_ffn_W1': _L0_ffn_in['W1'], 'L0_ffn_b1': _L0_ffn_in['b1'], 'L0_ffn_W2': _L0_ffn_in['W2'], 'L0_ffn_b2': _L0_ffn_in['b2']}

def reference(x, L0_conv_w_qk, L0_conv_g_qk, L0_conv_b_qk, L0_conv_m_qk, L0_conv_v_qk, L0_conv_w_v, L0_conv_g_v, L0_conv_b_v, L0_conv_m_v, L0_conv_v_v, L0_conv_w_p, L0_conv_g_p, L0_conv_b_p, L0_conv_m_p, L0_conv_v_p, L0_ffn_Wr, L0_ffn_br, L0_ffn_ln_g, L0_ffn_ln_b, L0_ffn_W1, L0_ffn_b1, L0_ffn_W2, L0_ffn_b2):
    import jax
    import jax.numpy as jnp

    def _L0_conv_ref(x, w_qk, g_qk, b_qk, m_qk, v_qk, w_v, g_v, b_v, m_v, v_v, w_p, g_p, b_p, m_p, v_p):
        import jax, jax.numpy as jnp
        import numpy as np
        NUM_HEADS = 8
        AREA = 4
        EPS = 1e-05

        def _conv1x1(x, w):
            return jnp.einsum('bchw,oc->bohw', x, w)

        def _bn(y, g, b, m, v):
            s = g / jnp.sqrt(v + EPS)
            return y * s[None, :, None, None] + (b - m * s)[None, :, None, None]
        B, C, H, W = x.shape
        N = H * W
        hd = C // NUM_HEADS
        qk = _bn(_conv1x1(x, w_qk), g_qk, b_qk, m_qk, v_qk)
        qk = qk.reshape(B, 2 * C, N).transpose(0, 2, 1)
        vv = _bn(_conv1x1(x, w_v), g_v, b_v, m_v, v_v)
        vv = vv.reshape(B, C, N).transpose(0, 2, 1)
        Ba, Na = (B * AREA, N // AREA)
        qk = qk.reshape(Ba, Na, 2 * C)
        vv = vv.reshape(Ba, Na, C)
        q, k = (qk[..., :C], qk[..., C:])
        q = q.reshape(Ba, Na, NUM_HEADS, hd).transpose(0, 2, 3, 1)
        k = k.reshape(Ba, Na, NUM_HEADS, hd).transpose(0, 2, 3, 1)
        v = vv.reshape(Ba, Na, NUM_HEADS, hd).transpose(0, 2, 3, 1)
        scale = hd ** (-0.5)
        attn = jnp.einsum('bhdi,bhdj->bhij', q, k) * scale
        attn = jax.nn.softmax(attn, axis=-1)
        out = jnp.einsum('bhdj,bhij->bihd', v, attn)
        out = out.reshape(B, N, C).reshape(B, H, W, C).transpose(0, 3, 1, 2)
        return _bn(_conv1x1(out, w_p), g_p, b_p, m_p, v_p)

    def _L0_ffn_ref(x, Wr, br, ln_g, ln_b, W1, b1, W2, b2):
        import jax, jax.numpy as jnp
        import numpy as np
        TOP_K = 2
        LN_EPS = 1e-05
        B, S, D = x.shape
        N = B * S
        xt = x.reshape(N, D)
        logits = xt @ Wr + br
        probs = jax.nn.softmax(logits, axis=-1)
        top_p, top_idx = jax.lax.top_k(probs, TOP_K)
        weights = top_p / top_p.sum(axis=-1, keepdims=True)
        mu = xt.mean(axis=-1, keepdims=True)
        var = ((xt - mu) ** 2).mean(axis=-1, keepdims=True)
        xn = (xt - mu) * jax.lax.rsqrt(var + LN_EPS)
        xe = xn[None, :, :] * ln_g[:, None, :] + ln_b[:, None, :]
        h = jax.nn.gelu(jnp.einsum('end,edh->enh', xe, W1) + b1[:, None, :], approximate=False)
        y = jnp.einsum('enh,ehd->end', h, W2) + b2[:, None, :]
        y_tok = jnp.transpose(y, (1, 0, 2))
        sel = jnp.take_along_axis(y_tok, top_idx[:, :, None], axis=1)
        out = (weights[:, :, None] * sel).sum(axis=1)
        return out.reshape(B, S, D)

    def _gn(v, G=32, eps=1e-05):
        B_, C_, H_, W_ = v.shape
        g = v.reshape(B_, G, C_ // G, H_, W_)
        m = jnp.mean(g, axis=(2, 3, 4), keepdims=True)
        s = jnp.var(g, axis=(2, 3, 4), keepdims=True)
        return ((g - m) / jnp.sqrt(s + eps)).reshape(v.shape)

    def _ln_c(v, eps=1e-06):
        m = jnp.mean(v, axis=1, keepdims=True)
        s = jnp.var(v, axis=1, keepdims=True)
        return (v - m) / jnp.sqrt(s + eps)

    def _ln_t(v, eps=1e-05):
        m = jnp.mean(v, axis=-1, keepdims=True)
        s = jnp.var(v, axis=-1, keepdims=True)
        return (v - m) / jnp.sqrt(s + eps)

    def _to_tokens(v):
        B_, C_, H_, W_ = v.shape
        return v.reshape(B_, C_, H_ * W_).transpose(0, 2, 1)

    def _from_tokens(t, like):
        B_, C_, H_, W_ = like.shape
        return t.transpose(0, 2, 1).reshape(B_, C_, H_, W_)
    x = x + _L0_conv_ref(_ln_c(x), L0_conv_w_qk, L0_conv_g_qk, L0_conv_b_qk, L0_conv_m_qk, L0_conv_v_qk, L0_conv_w_v, L0_conv_g_v, L0_conv_b_v, L0_conv_m_v, L0_conv_v_v, L0_conv_w_p, L0_conv_g_p, L0_conv_b_p, L0_conv_m_p, L0_conv_v_p)
    t = _to_tokens(x)
    t = t + _L0_ffn_ref(_ln_t(t), L0_ffn_Wr, L0_ffn_br, L0_ffn_ln_g, L0_ffn_ln_b, L0_ffn_W1, L0_ffn_b1, L0_ffn_W2, L0_ffn_b2)
    x = _from_tokens(t, x)
    return x

_drawn_inputs = setup_inputs


def setup_inputs(seed=0):
    import zlib

    import numpy as np

    out = dict(_drawn_inputs(seed))
    spreads = {'L0_ffn_br': (0.0, 0.1),
     'L0_ffn_ln_g': (1.0, 0.2),
     'L0_ffn_ln_b': (0.0, 0.1),
     'L0_ffn_b1': (0.0, 0.1),
     'L0_ffn_b2': (0.0, 0.1)}
    factors = {'L0_conv_b_qk': 7.008,
     'L0_conv_m_qk': 15.698,
     'L0_conv_v_qk': 18.074,
     'L0_conv_g_qk': 6.104}
    for name, (base, spread) in spreads.items():
        noise = np.random.default_rng([zlib.crc32(name.encode()), seed]).standard_normal(out[name].shape)
        drawn = base * np.exp(spread * noise) if base else spread * noise
        out[name] = jnp.asarray(drawn.astype(out[name].dtype))
    for name, factor in factors.items():
        out[name] = (out[name] * factor).astype(out[name].dtype)
    return out
```

```python
from contextlib import ExitStack

import numpy as np
import concourse.bass as bass
from concourse import mybir

F32 = mybir.dt.float32
F32R = mybir.dt.float32r
U32 = mybir.dt.uint32
ALU = mybir.AluOpType
ACT = mybir.ActivationFunctionType
AX = mybir.AxisListType

P = 128
B, C, N = 2, 64, 256
HEADS, HD = 8, 8
AREAS = 4
T = N // AREAS
HALVES = 2
NH = N // HALVES
AH = AREAS // HALVES
HP = HEADS // 2
E, HID = 8, 256
CH = E * HID // P
CE = HID // P
EP = E // 2
EPS_BN, EPS_C, EPS_T = 1e-5, 1e-6, 1e-5

CENTER = 0
IDENT = CENTER + P
MEAN_B = IDENT + P
MEAN_D = MEAN_B + 2
HMASK = MEAN_D + 1
IOTA = HMASK + HEADS
NEGHALF = IOTA + E
QSCALE = NEGHALF + 4
FOLD = QSCALE + 8
NCONST = FOLD + C

GAMMA, BETA, MEAN, VAR = 0, 4, 8, 12
LNG = 16
LNB = LNG + E
B2 = LNB + E
B1 = B2 + EP
BR = B1 + CH
WR = BR + E
NPAR = WR + E

H_RING, G_RING = 3, 6
LAG = 2
WARM = 12


def metaformer(nc, x_split, x_double, consts, params, wqkv, wproj, w1, w2, out):
    ctx = ExitStack()
    with ctx:
        def sb(name, shape, dt=F32):
            return ctx.enter_context(nc.sbuf_tensor(name, shape, dt))

        def sem(name):
            return ctx.enter_context(nc.semaphore(name))

        xs = sb("xs", [P, N])
        xd = sb("xd", [P, B, N])
        cst = sb("cst", [P, NCONST])
        par = sb("par", [P, NPAR])
        wq = sb("wq", [P, 3, P])
        wp = sb("wp", [P, B, P])
        w1s = sb("w1s", [P, E * HID])
        w2s = sb("w2s", [P, CH, C])
        warm = sb("warm", [P, 512])
        xc = sb("xc", [P, N])
        sq = sb("sq", [P, N])
        vare = sb("vare", [P, HALVES, B])
        rstd = sb("rstd", [P, HALVES, B])
        rstdw = sb("rstdw", [P, HALVES, B, C])
        xn = sb("xn", [P, N])
        kaff = sb("kaff", [P, N])
        kmask = sb("kmask", [P, AREAS, HEADS, T])
        qblk = sb("qblk", [P, AREAS, B, T])
        vblk = sb("vblk", [P, AREAS * HP, 32])
        bnv = sb("bnv", [P, 4])
        bnr = sb("bnr", [P, 4])
        bnst0 = sb("bnst0", [P, 8])
        bnms = sb("bnms", [P, 4])
        bnst = sb("bnst", [P, 8])
        ptot = sb("ptot", [P, 1])
        xt = sb("xt", [P, B, N])
        negmax = sb("rowmax", [P, 2, HEADS])
        sdif = sb("sdif", [P, 2, HEADS, T])
        prob = sb("prob", [P, 2, HEADS * T])
        rsum = sb("rsum", [P, AREAS, HEADS])
        rz = sb("rz", [P, AREAS, HEADS])
        rzw = sb("rzw", [P, 2, HEADS, P // HEADS])
        probT = sb("probT", [P, 2, HP, P])
        rzs = sb("rzs", [P, HALVES, AH * P])
        on = sb("on", [P, HALVES, AH, B, T])
        x1 = sb("x1", [P, HALVES, B, NH])
        xc2 = sb("xc2", [P, HALVES, B, NH])
        sq2 = sb("sq2", [P, HALVES, B, NH])
        var2 = sb("var2", [P, HALVES, 2, B])
        rstd2 = sb("rstd2", [P, HALVES, 2, B])
        rstdw2 = sb("rstdw2", [P, HALVES, B, P])
        xn2 = sb("xn2", [P, HALVES, B * NH])
        xr = sb("xr", [P, HALVES, B * NH], F32R)
        lgs = sb("lgs", [P, HALVES, B, E])
        lg = sb("lg", [P, HALVES, B, E])
        top = sb("top", [P, HALVES, B, 8])
        topi = sb("topi", [P, HALVES, B, 8], U32)
        dif = sb("dif", [P, HALVES, B])
        th = sb("th", [P, HALVES, B])
        g12 = sb("g12", [P, HALVES, 2, B])
        eq = sb("eq", [P, HALVES, 2, B, E])
        gate = sb("gate", [P, B, E, C])
        gateT = sb("gateT", [P, HALVES, EP, B * NH])
        w1hi = sb("w1hi", [P, E * HID], F32R)
        w1lo = sb("w1lo", [P, E * HID], F32R)
        w1g = sb("w1g", [P, 2, HID])
        cb = sb("cb", [P, CH])
        hg = sb("hg", [P, G_RING, B * NH])
        yg = sb("yg", [P, 2, B * NH])
        acc = sb("acc", [P, HALVES, B * NH])
        res = sb("res", [C, HALVES, B, NH])
        tiny = sb("tiny", [P, 1])

        bank = [ctx.enter_context(nc.psum_tensor(f"bank{i}", [P, 512], F32)) for i in range(8)]
        XC = [bank[7], bank[6]]
        VARB = [bank[5], bank[4]]
        RB = [bank[3], bank[2]]
        QP = [bank[0], bank[4]]
        KP = [bank[1], bank[5]]
        VP = [bank[7], bank[6]]
        S = [bank[0], bank[1]]
        PT = [bank[2], bank[3]]
        OT = [bank[4], bank[5]]
        RZ = bank[6]
        MISC = bank[7]
        ROUT = [bank[4], bank[5]]
        GATE = [bank[4], bank[5]]
        H = [bank[0], bank[1], bank[2]]
        Y = [bank[3], bank[6]]
        FIN = [bank[4], bank[5]]

        ident = cst[:, IDENT:IDENT + P]

        (l_xs, l_cst, l_par, l_wq, l_wp, l_xd, l_w1a, l_w1b, l_w2) = (
            sem("l_" + n) for n in ("xs", "cst", "par", "wq", "wp", "xd", "w1a", "w1b", "w2"))
        stored = sem("stored")
        (p_xc, p_var, p_rb, p_q, p_k, p_v, p_pt, p_s, p_t, p_o, p_rz, p_cb, p_proj, p_xc2, p_var2,
         p_rb2, p_lg, p_gate, p_h, p_y, p_fin) = (sem("p_" + n) for n in (
            "xc", "var", "rb", "q", "k", "v", "ptot", "s", "t", "o", "rz", "cb", "proj", "xc2",
            "var2", "rb2", "lg", "gate", "h", "y", "fin"))
        (a_sq, a_q, a_v, a_p, a_pt, a_rzs, a_sq2, a_th, a_g) = (sem("a_" + n) for n in (
            "sq", "q", "v", "prob", "probT", "rzs", "sq2", "tanh", "gelu"))
        (v_xc, v_vare, v_xn, v_bn, v_kaff, v_kmask, v_ptot, v_xt, v_max, v_sub, v_sum, v_rz, v_on,
         v_x1, v_xc2, v_var2, v_xn2, v_hi, v_lo, v_lg, v_top, v_g12, v_eq, v_gate, v_gateT, v_w1lo,
         v_cb, v_yg, v_acc, v_res, v_rstdw, v_rzw, v_rstdw2) = (sem("v_" + n) for n in (
            "xc", "vare", "xn", "bn", "kaff", "kmask", "ptot", "xt", "max", "sub", "sum", "rz",
            "on", "x1", "xc2", "var2", "xn2", "hi", "lo", "lg", "top", "g12", "eq", "gate",
            "gateT", "w1lo", "cb", "yg", "acc", "res", "rstdw", "rzw", "rstdw2"))
        (g_warm, g_zero, g_rstd, g_bnr, g_kmask, g_w1hi, g_w1g, g_w1lo, g_rstd2) = (
            sem("g_" + n) for n in (
                "warm", "zero", "rstd", "bnr", "kmask", "w1hi", "w1g", "w1lo", "rstd2"))

        K_DVE = 2
        LO_POOL = 4

        block = ctx.enter_context(nc.Block())

        @block.sync
        def _(sp):
            sp.dma_start(xs[:, :], x_split).then_inc(l_xs, 16)
            sp.dma_start(par[:, :], params).then_inc(l_par, 16)
            sp.dma_start(w1s[0:C, :], w1).then_inc(l_w1a, 16)
            sp.dma_start(w1s[C:P, :], w1).then_inc(l_w1b, 16)
            for f in range(HALVES):
                sp.wait_ge(v_res, f + 1)
                sp.dma_start(out[f], res[:, f]).then_inc(stored, 16)
            sp.wait_ge(stored, 16 * HALVES)

        @block.gpsimd
        def _(pool):
            pool.memset(warm[:, :], 0.0).then_inc(g_warm, 1)
            pool.memset(qblk[:, :, :, :], 0.0).then_inc(g_zero, 1)
            pool.memset(vblk[:, :, :], 0.0).then_inc(g_zero, 1)
            pool.wait_ge(l_cst, 16)
            pool.wait_ge(v_bn, 1)
            pool.tensor_tensor(bnr[:, :], bnv[:, :], cst[:, NEGHALF:NEGHALF + 4], ALU.pow)\
                .then_inc(g_bnr, 1)
            for f in range(HALVES):
                pool.wait_ge(v_vare, f + 1)
                pool.tensor_tensor(rstd[:, f], vare[:, f], cst[:, NEGHALF:NEGHALF + B], ALU.pow)\
                    .then_inc(g_rstd, 1)
            pool.wait_ge(l_par, 16)
            pool.wait_ge(l_w1a, 16)
            pool.wait_ge(l_w1b, 16)

            def w1_hi(e):
                cols = slice(e * HID, (e + 1) * HID)
                pool.tensor_scalar(w1hi[:, cols], w1s[:, cols], par[:, LNG + e:LNG + e + 1], 1.0,
                                   ALU.mult, ALU.mult).then_inc(g_w1hi, 1)

            def w1_g(e):
                if e >= 2:
                    pool.wait_ge(g_w1lo, e - 1)
                cols = slice(e * HID, (e + 1) * HID)
                pool.tensor_scalar(w1g[:, e % 2], w1s[:, cols], par[:, LNG + e:LNG + e + 1], 1.0,
                                   ALU.mult, ALU.mult).then_inc(g_w1g, 1)

            def w1_lo(e):
                cols = slice(e * HID, (e + 1) * HID)
                pool.wait_ge(g_w1g, e + 1)
                pool.wait_ge(g_w1hi, e + 1)
                pool.tensor_tensor(w1lo[:, cols], w1g[:, e % 2], w1hi[:, cols].bitcast(F32),
                                   ALU.subtract).then_inc(g_w1lo, 1)

            def norm2(f):
                for i in range(2):
                    pool.wait_ge(v_var2, 2 * f + i + 1)
                    pool.tensor_tensor(rstd2[:, f, i], var2[:, f, i],
                                       cst[:, NEGHALF:NEGHALF + B], ALU.pow).then_inc(g_rstd2, 1)

            for a in range(K_DVE, AREAS):
                pool.wait_ge(v_kaff, a // AH + 1)
                pool.tensor_tensor(
                    kmask[:, a], kaff[:, None, a * T:(a + 1) * T].broadcast_to((P, HEADS, T)),
                    cst[:, HMASK:HMASK + HEADS, None].broadcast_to((P, HEADS, T)), ALU.mult)\
                    .then_inc(g_kmask, 1)
            for e in range(E):
                w1_hi(e)
            w1_g(0)
            for e in range(LO_POOL):
                if e + 1 < LO_POOL:
                    w1_g(e + 1)
                w1_lo(e)
            norm2(0)
            norm2(1)

        @block.scalar
        def _(act):
            act.dma_start(cst[:, :], consts).then_inc(l_cst, 16)
            act.dma_start(wq[:, :, :], wqkv).then_inc(l_wq, 16)
            act.dma_start(wp[:, :, :], wproj).then_inc(l_wp, 16)
            act.dma_start(xd[:, :, :], x_double).then_inc(l_xd, 16)
            act.dma_start(w2s[:, :, :], w2).then_inc(l_w2, 16)
            act.wait_ge(g_warm, 1)
            act.activation(tiny[:, :], warm[:, 0:1], ACT.Exp)
            act.wait_ge(p_xc, 1)
            act.activation(sq[:, 0:NH], XC[0][:, 0:NH], ACT.Square).then_inc(a_sq, 1)
            act.wait_ge(v_xc, 1)
            act.activation(sq[:, NH:N], XC[1][:, 0:NH], ACT.Square).then_inc(a_sq, 1)
            act.wait_ge(v_bn, 5)
            act.wait_ge(g_zero, 2)
            for f in range(HALVES):
                act.wait_ge(p_q, f + 1)
                for b in range(B):
                    rows = slice(b * C, (b + 1) * C)
                    act.activation(qblk[rows, AH * f:AH * (f + 1), b, :],
                                   QP[f][rows, 0:NH].rearrange("p (a i) -> p a i", a=AH),
                                   ACT.Identity, bias=bnst[rows, 4:5], scale=bnst[rows, 0:1])\
                        .then_inc(a_q, 1)
                act.wait_ge(p_v, f + 1)
                for h in range(2):
                    rows, cols = slice(h * T, (h + 1) * T), slice(16 * h, 16 * h + 16)
                    act.activation(vblk[rows, AH * HP * f:AH * HP * (f + 1), cols],
                                   VP[f][rows, 0:AH * P].rearrange("p (a c) -> p a c", c=32)[:, :, cols],
                                   ACT.Copy).then_inc(a_v, 1)

            def exp(a):
                act.wait_ge(v_sub, a + 1)
                if a >= 2:
                    act.wait_ge(p_t, a - 1)
                    act.wait_ge(v_sum, a - 1)
                act.activation(prob[:, a % 2, :], sdif[:, a % 2].rearrange("p h j -> p (h j)"),
                               ACT.Exp).then_inc(a_p, 1)

            def turned(a):
                act.wait_ge(p_t, a + 1)
                if a >= 2:
                    act.wait_ge(p_o, a - 1)
                act.activation(probT[:, a % 2].rearrange("p h i -> p (h i)"), PT[a % 2][:, :],
                               ACT.Copy).then_inc(a_pt, 1)

            def inverse_sums(f):
                act.wait_ge(p_rz, AH * (f + 1))
                act.activation(rzs[:, f, :], RZ[:, f * AH * P:(f + 1) * AH * P], ACT.Copy,
                               scale=bnst[:, 2:3]).then_inc(a_rzs, 1)

            def squares2(f):
                act.wait_ge(p_xc2, f + 1)
                act.activation(sq2[:, f].rearrange("p b n -> p (b n)"), MISC[:, 0:B * NH],
                               ACT.Square).then_inc(a_sq2, 1)

            def tanh(f):
                act.wait_ge(v_top, 5 * f + 5)
                act.activation(th[:, f, :], dif[:, f, :], ACT.Tanh, scale=0.5).then_inc(a_th, 1)

            def gelu(f, c):
                n = f * CH + c
                if n == 0:
                    act.wait_ge(v_cb, 1)
                act.wait_ge(p_h, n + 1)
                if n >= G_RING:
                    act.wait_ge(p_y, n - G_RING + 1)
                act.activation(hg[:, n % G_RING, :], H[n % H_RING][:, 0:B * NH], ACT.Gelu,
                               bias=cb[:, c:c + 1]).then_inc(a_g, 1)

            exp(0)
            turned(0)
            exp(1)
            turned(1)
            exp(2)
            inverse_sums(0)
            turned(2)
            exp(3)
            squares2(0)
            turned(3)
            inverse_sums(1)
            act.activation(tiny[:, :], warm[:, 0:1], ACT.Gelu)
            for f in range(HALVES):
                for c in range(CH):
                    if f == 0 and c == 3:
                        squares2(1)
                    if c == 1 and f == 0:
                        tanh(0)
                    if c == 9 and f == 0:
                        tanh(1)
                    gelu(f, c)

        @block.vector
        def _(dve):
            dve.wait_ge(l_par, 16)
            dve.tensor_scalar(bnv[:, :], par[:, VAR:VAR + 4], EPS_BN, None, ALU.add).then_inc(v_bn, 1)
            dve.wait_ge(p_xc, 2)
            dve.tensor_copy(xc[:, NH:N], XC[1][:, 0:NH]).then_inc(v_xc, 1)
            dve.wait_ge(a_sq, 1)
            dve.tensor_copy(xc[:, 0:NH], XC[0][:, 0:NH]).then_inc(v_xc, 1)
            dve.wait_ge(g_bnr, 1)
            dve.tensor_tensor(bnst0[:, 0:4], par[:, GAMMA:GAMMA + 4], bnr[:, :], ALU.mult)\
                .then_inc(v_bn, 1)
            for f in range(HALVES):
                dve.wait_ge(p_var, f + 1)
                dve.tensor_scalar(vare[:, f, :], VARB[f][:, 0:B], EPS_C, None, ALU.add)\
                    .then_inc(v_vare, 1)
            dve.wait_ge(v_bn, 2)
            dve.tensor_tensor(bnms[:, :], par[:, MEAN:MEAN + 4], bnst0[:, 0:4], ALU.mult)\
                .then_inc(v_bn, 1)
            dve.wait_ge(v_bn, 3)
            dve.tensor_tensor(bnst0[:, 4:8], par[:, BETA:BETA + 4], bnms[:, :], ALU.subtract)\
                .then_inc(v_bn, 1)
            dve.wait_ge(v_bn, 4)
            dve.wait_ge(l_cst, 16)
            dve.tensor_tensor(bnst[:, :], bnst0[:, :], cst[:, QSCALE:QSCALE + 8], ALU.mult)\
                .then_inc(v_bn, 1)
            dve.wait_ge(v_xc, 2)
            for f in range(HALVES):
                dve.wait_ge(g_rstd, f + 1)
                dve.tensor_copy(rstdw[:, f], rstd[:, f, :, None].broadcast_to((P, B, C))).then_inc(v_rstdw, 1)
            for f in range(HALVES):
                dve.wait_ge(p_rb, f + 1)
                dve.tensor_tensor(xn[:, f * NH:(f + 1) * NH], xc[:, f * NH:(f + 1) * NH],
                                  RB[f][:, 0:NH], ALU.mult).then_inc(v_xn, 1)
            dve.wait_ge(v_bn, 5)

            def k_affine(f):
                dve.wait_ge(p_k, f + 1)
                dve.tensor_scalar(kaff[:, f * NH:(f + 1) * NH], KP[f][:, 0:NH], bnst[:, 1:2],
                                  bnst[:, 5:6], ALU.mult, ALU.add).then_inc(v_kaff, 1)

            def k_masked(a):
                dve.wait_ge(v_kaff, a // AH + 1)
                dve.tensor_tensor(
                    kmask[:, a], kaff[:, None, a * T:(a + 1) * T].broadcast_to((P, HEADS, T)),
                    cst[:, HMASK:HMASK + HEADS, None].broadcast_to((P, HEADS, T)), ALU.mult)\
                    .then_inc(v_kmask, 1)

            def score_max(a):
                dve.wait_ge(p_s, a + 1)
                dve.tensor_reduce(negmax[:, a % 2, :], S[a % 2][:, :].rearrange("p (h j) -> p h j", h=HEADS),
                                  AX.X, ALU.max).then_inc(v_max, 1)

            def score_sub(a):
                dve.wait_ge(v_max, a + 1)
                if a >= 2:
                    dve.wait_ge(a_p, a - 1)
                dve.tensor_tensor(sdif[:, a % 2], S[a % 2][:, :].rearrange("p (h j) -> p h j", h=HEADS),
                                  negmax[:, a % 2, :, None].broadcast_to((P, HEADS, T)),
                                  ALU.subtract).then_inc(v_sub, 1)

            def prob_sum(a):
                dve.wait_ge(a_p, a + 1)
                dve.tensor_reduce(rsum[:, a, :], prob[:, a % 2, :].rearrange("p (h j) -> p h j", h=HEADS),
                                  AX.X, ALU.add).then_inc(v_sum, 1)

            def prob_inverse(a):
                dve.wait_ge(v_sum, a + 1)
                dve.reciprocal(rz[:, a, :], rsum[:, a, :]).then_inc(v_rz, 1)
                dve.wait_ge(v_rz, a + 1)
                if a >= 2:
                    dve.wait_ge(p_rz, a - 1)
                dve.tensor_copy(rzw[:, a % 2], rz[:, a, :, None].broadcast_to((P, HEADS, P // HEADS)))\
                    .then_inc(v_rzw, 1)

            def normalise(f):
                dve.wait_ge(p_o, AH * (f + 1))
                dve.wait_ge(a_rzs, f + 1)
                dve.tensor_tensor(on[:, f].rearrange("p a b i -> p (a b i)"), OT[f][:, 0:AH * P],
                                  rzs[:, f, :], ALU.mult).then_inc(v_on, 1)

            def residual(f):
                dve.wait_ge(p_proj, f + 1)
                dve.wait_ge(v_xt, 1)
                dve.scalar_tensor_tensor(out=x1[:, f], in0=MISC[:, 0:B * NH].rearrange("p (b n) -> p b n", b=B),
                                         scalar=bnst[:, 3:4], in1=xt[:, :, f * NH:(f + 1) * NH],
                                         op0=ALU.mult, op1=ALU.add).then_inc(v_x1, 1)

            def centred2(f):
                dve.wait_ge(a_sq2, f + 1)
                dve.tensor_copy(xc2[:, f].rearrange("p b n -> p (b n)"), MISC[:, 0:B * NH])\
                    .then_inc(v_xc2, 1)

            def variance2(f):
                dve.wait_ge(p_var2, f + 1)
                dve.tensor_scalar(var2[:, f, 0, :], ROUT[f][:, 0:B], 1.0 + EPS_T, EPS_T * EPS_T,
                                  ALU.mult, ALU.add).then_inc(v_var2, 1)
                dve.tensor_scalar(var2[:, f, 1, :], ROUT[f][:, 0:B], EPS_T, None, ALU.add)\
                    .then_inc(v_var2, 1)

            def spread2(f):
                dve.wait_ge(g_rstd2, 2 * f + 1)
                dve.tensor_copy(rstdw2[:, f], rstd2[:, f, 0, :, None].broadcast_to((P, B, P)))\
                    .then_inc(v_rstdw2, 1)

            def normed2(f):
                dve.wait_ge(p_rb2, f + 1)
                dve.wait_ge(v_xc2, f + 1)
                dve.tensor_tensor(xn2[:, f, :], xc2[:, f].rearrange("p b n -> p (b n)"),
                                  MISC[:, 0:B * NH], ALU.mult).then_inc(v_xn2, 1)
                dve.wait_ge(v_xn2, f + 1)
                dve.tensor_copy(xr[:, f, :], xn2[:, f, :]).then_inc(v_hi, 1)
                dve.wait_ge(v_hi, f + 1)
                dve.tensor_tensor(xr[C:P, f, :], xn2[C:P, f, :], xr[C:P, f, :].bitcast(F32),
                                  ALU.subtract).then_inc(v_lo, 1)

            def router(f):
                dve.wait_ge(p_lg, f + 1)
                dve.wait_ge(g_rstd2, 2 * f + 2)
                dve.tensor_tensor(lgs[:, f], ROUT[f][:, 64:64 + B * E].rearrange("p (b e) -> p b e", b=B),
                                  rstd2[:, f, 1, :, None].broadcast_to((P, B, E)), ALU.mult)\
                    .then_inc(v_lg, 1)
                dve.wait_ge(v_lg, 2 * f + 1)
                dve.tensor_tensor(lg[:, f], lgs[:, f], par[:, None, BR:BR + E].broadcast_to((P, B, E)),
                                  ALU.add).then_inc(v_lg, 1)
                dve.wait_ge(v_lg, 2 * f + 2)
                for b in range(B):
                    dve.max(top[:, f, b, :], lg[:, f, b, :]).then_inc(v_top, 1)
                dve.wait_ge(v_top, 5 * f + 2)
                for b in range(B):
                    dve.max_index(topi[:, f, b, :], top[:, f, b, :], lg[:, f, b, :]).then_inc(v_top, 1)
                dve.tensor_tensor(dif[:, f, :], top[:, f, :, 0], top[:, f, :, 1], ALU.subtract)\
                    .then_inc(v_top, 1)
                dve.wait_ge(v_top, 5 * f + 5)
                for i in range(2):
                    dve.tensor_tensor(eq[:, f, i], cst[:, None, IOTA:IOTA + E].broadcast_to((P, B, E)),
                                      topi[:, f, :, i:i + 1].broadcast_to((P, B, E)), ALU.is_equal)\
                        .then_inc(v_eq, 1)

            def gates(f):
                dve.wait_ge(a_th, f + 1)
                dve.tensor_scalar(g12[:, f, 0, :], th[:, f, :], 0.5, 0.5, ALU.mult, ALU.add)\
                    .then_inc(v_g12, 1)
                dve.tensor_scalar(g12[:, f, 1, :], th[:, f, :], -0.5, 0.5, ALU.mult, ALU.add)\
                    .then_inc(v_g12, 1)
                dve.wait_ge(v_g12, 2 * f + 2)
                for i in range(2):
                    dve.wait_ge(v_eq, 4 * f + 2)
                    dve.tensor_tensor(eq[:, f, i], eq[:, f, i],
                                      g12[:, f, i, :, None].broadcast_to((P, B, E)), ALU.mult)\
                        .then_inc(v_eq, 1)
                dve.wait_ge(v_eq, 4 * f + 4)
                if f == 1:
                    dve.wait_ge(p_gate, 2)
                dve.tensor_tensor(gate[:, :, :, :], eq[:, f, 0, :, :, None].broadcast_to((P, B, E, C)),
                                  eq[:, f, 1, :, :, None].broadcast_to((P, B, E, C)), ALU.add)\
                    .then_inc(v_gate, 1)

            def gates_turned(f, i):
                dve.wait_ge(p_gate, 2 * f + i + 1)
                dve.tensor_copy(gateT[:, f, 2 * i:2 * i + 2, :].rearrange("p e n -> p (e n)"),
                                GATE[f][:, :]).then_inc(v_gateT, 1)

            def w1_lo(e):
                cols = slice(e * HID, (e + 1) * HID)
                dve.wait_ge(g_w1hi, e + 1)
                dve.scalar_tensor_tensor(out=w1lo[:, cols], in0=w1s[:, cols],
                                         scalar=par[:, LNG + e:LNG + e + 1],
                                         in1=w1hi[:, cols].bitcast(F32), op0=ALU.mult,
                                         op1=ALU.subtract).then_inc(v_w1lo, 1)

            def mix(f, p):
                n = f * EP + p
                dve.wait_ge(p_y, f * CH + 2 * CE * (p + 1))
                dve.wait_ge(v_gateT, 2 * f + p // 2 + 1)
                dst = acc[:, f, :] if p == 0 else yg[:, p % 2, :]
                dve.scalar_tensor_tensor(out=dst, in0=Y[n % 2][:, 0:B * NH], scalar=par[:, B2 + p:B2 + p + 1],
                                         in1=gateT[:, f, p, :], op0=ALU.add, op1=ALU.mult)\
                    .then_inc(v_yg, 1)
                dve.wait_ge(v_yg, n + 1)
                if p > 0:
                    if p > 1:
                        dve.wait_ge(v_acc, f * (EP - 1) + p - 1)
                    dve.tensor_tensor(acc[:, f, :], acc[:, f, :], yg[:, p % 2, :], ALU.add)\
                        .then_inc(v_acc, 1)

            def result(f):
                dve.wait_ge(p_fin, f + 1)
                dve.tensor_tensor(res[:, f].rearrange("p b n -> p (b n)"), FIN[f][0:C, 0:B * NH],
                                  x1[0:C, f].rearrange("p b n -> p (b n)"), ALU.add).then_inc(v_res, 1)

            k_affine(0)
            k_masked(0)
            k_affine(1)
            score_max(0)
            score_sub(0)
            k_masked(1)
            dve.wait_ge(p_pt, 1)
            dve.tensor_scalar(ptot[:, :], MISC[:, 384:385], bnst[:, 3:4], bnst[:, 7:8], ALU.mult, ALU.add)\
                .then_inc(v_ptot, 1)
            score_max(1)
            score_sub(1)
            prob_sum(0)
            prob_inverse(0)
            dve.wait_ge(l_xd, 16)
            dve.wait_ge(v_ptot, 1)
            dve.tensor_scalar(xt[:, :, :].rearrange("p b n -> p (b n)"), xd[:, :, :].rearrange("p b n -> p (b n)"),
                              ptot[:, 0:1], None, ALU.add).then_inc(v_xt, 1)
            score_max(2)
            score_sub(2)
            prob_sum(1)
            prob_inverse(1)
            dve.wait_ge(p_cb, 1)
            dve.tensor_tensor(cb[:, :], MISC[:, 400:400 + CH], par[:, B1:B1 + CH], ALU.add)\
                .then_inc(v_cb, 1)
            normalise(0)
            score_max(3)
            score_sub(3)
            residual(0)
            prob_sum(2)
            prob_inverse(2)
            variance2(0)
            centred2(0)
            prob_sum(3)
            prob_inverse(3)
            spread2(0)
            normed2(0)
            for e in range(LO_POOL, E):
                w1_lo(e)
            router(0)
            normalise(1)
            gates(0)
            residual(1)
            variance2(1)
            centred2(1)
            gates_turned(0, 0)
            gates_turned(0, 1)
            spread2(1)
            normed2(1)
            mix(0, 0)
            router(1)
            mix(0, 1)
            gates(1)
            mix(0, 2)
            gates_turned(1, 0)
            gates_turned(1, 1)
            mix(0, 3)
            result(0)
            for p in range(EP):
                mix(1, p)
            result(1)

        @block.tensor
        def _(pe):
            pe.wait_ge(g_warm, 1)
            for _ in range(WARM):
                pe.matmul(bank[0][:, :], warm[:, 0:P], warm[:, :], start=True, stop=True)
            pe.wait_ge(l_xs, 16)
            pe.wait_ge(l_cst, 16)
            for f in range(HALVES):
                pe.matmul(XC[f][:, 0:NH], cst[:, CENTER:CENTER + P], xs[:, f * NH:(f + 1) * NH],
                          start=True, stop=True).then_inc(p_xc, 1)
            for f in range(HALVES):
                pe.wait_ge(a_sq, f + 1)
                pe.matmul(VARB[f][:, 0:B], sq[:, f * NH:(f + 1) * NH], cst[:, MEAN_B:MEAN_B + B],
                          start=True, stop=True).then_inc(p_var, 1)
            for f in range(HALVES):
                pe.wait_ge(v_rstdw, f + 1)
                pe.transpose(RB[f][:, 0:NH], rstdw[:, f].rearrange("p b c -> p (b c)"), ident)\
                    .then_inc(p_rb, 1)
            pe.wait_ge(l_wq, 16)
            for f in range(HALVES):
                pe.wait_ge(v_xn, f + 1)
                x_f = xn[:, f * NH:(f + 1) * NH]
                if f == 1:
                    pe.wait_ge(v_vare, 2)
                pe.matmul(KP[f][:, 0:NH], wq[:, 1, :], x_f, start=True, stop=True).then_inc(p_k, 1)
                pe.matmul(QP[f][:, 0:NH], wq[:, 0, :], x_f, start=True, stop=True).then_inc(p_q, 1)
                if f == 0:
                    pe.wait_ge(v_xc, 2)
                    pe.wait_ge(a_sq, 2)
                for i in range(AH):
                    tok = xn[:, (AH * f + i) * T:(AH * f + i + 1) * T]
                    for h in range(2):
                        mm = pe.matmul(VP[f][h * T:(h + 1) * T, i * P:(i + 1) * P], tok, wq[:, 2, :],
                                       start=True, stop=True)
                mm.then_inc(p_v, 1)

            def scores(a):
                if a < 2:
                    pe.wait_ge(a_q, 2 * B if a == 1 and AH == 1 else B)
                    pe.wait_ge(v_kaff, 1)
                if a >= 2:
                    pe.wait_ge(a_q, 2 * B)
                    pe.wait_ge(v_sub, a - 1)
                if a < K_DVE:
                    pe.wait_ge(v_kmask, a + 1)
                else:
                    pe.wait_ge(g_kmask, a - K_DVE + 1)
                pe.matmul(S[a % 2][:, :], qblk[:, a].rearrange("p b i -> p (b i)"),
                          kmask[:, a].rearrange("p h j -> p (h j)"), start=True, stop=True)\
                    .then_inc(p_s, 1)

            def turn(a):
                pe.wait_ge(a_p, a + 1)
                if a < 2:
                    pe.wait_ge(v_xn, 2)
                else:
                    pe.wait_ge(a_pt, a - 1)
                for h in range(HP):
                    mm = pe.transpose(PT[a % 2][:, h * P:(h + 1) * P], prob[:, a % 2, h * P:(h + 1) * P], ident)
                mm.then_inc(p_t, 1)

            def attend(a):
                f, i = a // AH, a % AH
                pe.wait_ge(a_pt, a + 1)
                pe.wait_ge(a_v, 2 * (f + 1))
                if a == 0:
                    pe.wait_ge(a_q, 2 * B)
                    pe.wait_ge(v_kaff, 2)
                for h in range(HP):
                    mm = pe.matmul(OT[f][32 * h:32 * h + 32, i * P:(i + 1) * P], vblk[:, a * HP + h, :],
                                   probT[:, a % 2, h, :], start=True, stop=True)
                mm.then_inc(p_o, 1)

            def inverse_rows(a):
                f = a // AH
                pe.wait_ge(v_rzw, a + 1)
                if a == 0:
                    pe.wait_ge(a_v, 2 * HALVES)
                if a == AH:
                    pe.wait_ge(a_rzs, 1)
                pe.transpose(RZ[:, a * P:(a + 1) * P], rzw[:, a % 2].rearrange("p h r -> p (h r)"), ident).then_inc(p_rz, 1)

            def shift_of_v():
                pe.wait_ge(l_wp, 16)
                pe.wait_ge(v_bn, 5)
                pe.wait_ge(a_v, 2)
                pe.matmul(MISC[:, 384:385], wp[:, 0, :], bnst[:, 6:7], start=True, stop=True)\
                    .then_inc(p_pt, 1)

            def expert_bias(c0, c1):
                if c0 == 0:
                    pe.wait_ge(l_w1a, 16)
                    pe.wait_ge(l_w1b, 16)
                    pe.wait_ge(v_ptot, 1)
                for c in range(c0, c1):
                    e = c // CE
                    mm = pe.matmul(MISC[:, 400 + c:401 + c], w1s[:, c * P:(c + 1) * P],
                                   par[:, LNB + e:LNB + e + 1], start=True, stop=True)
                if c1 == CH:
                    mm.then_inc(p_cb, 1)

            def project(f):
                pe.wait_ge(v_on, f + 1)
                if f == 0:
                    pe.wait_ge(v_cb, 1)
                else:
                    pe.wait_ge(v_xn2, 1)
                for b in range(B):
                    mm = pe.matmul(MISC[:, b * NH:(b + 1) * NH], wp[:, b, :], on[:, f, :, b, :],
                                   start=True, stop=True)
                mm.then_inc(p_proj, 1)

            def centre2(f):
                pe.wait_ge(v_x1, f + 1)
                pe.matmul(MISC[:, 0:B * NH], cst[:, CENTER:CENTER + P],
                          x1[:, f].rearrange("p b n -> p (b n)"), start=True, stop=True).then_inc(p_xc2, 1)

            def var2_rows(f):
                pe.wait_ge(a_sq2, f + 1)
                for b in range(B):
                    mm = pe.matmul(ROUT[f][:, b:b + 1], sq2[:, f, b, :], cst[:, MEAN_D:MEAN_D + 1],
                                   start=True, stop=True)
                mm.then_inc(p_var2, 1)

            def spread2(f):
                pe.wait_ge(v_rstdw2, f + 1)
                pe.wait_ge(v_xc2, f + 1)
                for b in range(B):
                    mm = pe.transpose(MISC[:, b * NH:(b + 1) * NH], rstdw2[:, f, b, :], ident)
                mm.then_inc(p_rb2, 1)

            def logits(f):
                pe.wait_ge(v_xc2, f + 1)
                pe.wait_ge(v_var2, 2 * f + 2)
                for b in range(B):
                    mm = pe.matmul(ROUT[f][:, 64 + b * E:64 + (b + 1) * E], xc2[:, f, b, :],
                                   par[:, WR:WR + E], start=True, stop=True)
                mm.then_inc(p_lg, 1)

            def gate_rows(f, i):
                if i == 0:
                    pe.wait_ge(v_gate, f + 1)
                else:
                    pe.wait_ge(v_gateT, 2 * f + 1)
                for p in range(2 * i, 2 * i + 2):
                    for b in range(B):
                        mm = pe.transpose(GATE[f][:, ((p % 2) * B + b) * NH:((p % 2) * B + b + 1) * NH],
                                          gate[:, b, 2 * p:2 * p + 2, :].rearrange("p e c -> p (e c)"), ident)
                mm.then_inc(p_gate, 1)

            def hidden(f, c):
                n = f * CH + c
                e = c // CE
                if f == 0 and c % CE == 0:
                    pe.wait_ge(g_w1hi, e + 1)
                    if e < LO_POOL:
                        pe.wait_ge(g_w1lo, e + 1)
                    else:
                        pe.wait_ge(v_w1lo, e - LO_POOL + 1)
                if c == 0:
                    pe.wait_ge(v_lo, f + 1)
                if n >= H_RING:
                    pe.wait_ge(a_g, n - H_RING + 1)
                pe.matmul(H[n % H_RING][:, 0:B * NH], w1hi[:, c * P:(c + 1) * P], xr[:, f, :],
                          start=True, stop=False)
                pe.matmul(H[n % H_RING][:, 0:B * NH], w1lo[:, c * P:(c + 1) * P], xr[:, f, :],
                          start=False, stop=True).then_inc(p_h, 1)

            def expert_out(f, c):
                n = f * CH + c
                e, half = c // CE, c % CE
                pair = f * EP + e // 2
                if n == 0:
                    pe.wait_ge(l_w2, 16)
                if c % (2 * CE) == 0 and pair >= 2:
                    pe.wait_ge(v_yg, pair - 1)
                if n == 2 * CE:
                    pe.wait_ge(a_rzs, 2)
                pe.wait_ge(a_g, n + 1)
                rows = slice(C * (e % 2), C * (e % 2) + C)
                pe.matmul(Y[pair % 2][rows, 0:B * NH], w2s[:, c, :], hg[:, n % G_RING, :],
                          start=(half == 0), stop=(half == CE - 1)).then_inc(p_y, 1)

            def sum_rows(f):
                pe.wait_ge(v_acc, (EP - 1) * (f + 1))
                pe.wait_ge(v_gateT, 2 * f + 2)
                pe.matmul(FIN[f][0:C, 0:B * NH], cst[:, FOLD:FOLD + C], acc[:, f, :], start=True, stop=True)\
                    .then_inc(p_fin, 1)

            scores(0)
            scores(1)
            shift_of_v()
            turn(0)
            expert_bias(0, 4)
            scores(2)
            attend(0)
            inverse_rows(0)
            expert_bias(4, 10)
            turn(1)
            expert_bias(10, CH)
            scores(3)
            attend(1)
            inverse_rows(1)
            turn(2)
            project(0)
            attend(2)
            inverse_rows(2)
            centre2(0)
            turn(3)
            var2_rows(0)
            attend(3)
            inverse_rows(3)
            logits(0)
            spread2(0)
            between = {
                (0, 1): [lambda: project(1)],
                (0, 2): [lambda: centre2(1), lambda: gate_rows(0, 0)],
                (0, 3): [lambda: var2_rows(1), lambda: gate_rows(0, 1)],
                (0, 5): [lambda: logits(1), lambda: spread2(1)],
                (0, 12): [lambda: gate_rows(1, 0)],
                (0, 14): [lambda: gate_rows(1, 1)],
                (1, 4): [lambda: sum_rows(0)],
            }
            steps = [(f, c) for f in range(HALVES) for c in range(CH)]
            for n, (f, c) in enumerate(steps):
                hidden(f, c)
                if n >= LAG:
                    expert_out(*steps[n - LAG])
                for piece in between.get((f, c), []):
                    piece()
            for step in steps[-LAG:]:
                expert_out(*step)
            sum_rows(1)


def shape_constants():
    c = np.zeros((P, NCONST), np.float32)
    row = np.arange(P)
    same = row[:, None] // C == row[None, :] // C
    c[:, CENTER:CENTER + P] = np.eye(P) - same / C
    c[:, IDENT:IDENT + P] = np.eye(P)
    c[:, MEAN_B:MEAN_B + B] = (row[:, None] // C == np.arange(B)) / C
    c[:, MEAN_D] = 1.0 / P
    c[:, HMASK:HMASK + HEADS] = (row[:, None] % C) // HD == np.arange(HEADS)
    c[:, IOTA:IOTA + E] = np.arange(E)
    c[:, NEGHALF:NEGHALF + 4] = -0.5
    c[:, QSCALE:QSCALE + 8] = 1.0
    c[:, [QSCALE, QSCALE + 4]] = HD ** -0.5
    c[:, FOLD:FOLD + C] = row[:, None] % C == np.arange(C)
    return c


def kernel(**inputs):
    import concourse.bacc as bacc
    from concourse.bass_utils import run_bass_kernel_spmd

    a = {k.replace("L0_", ""): np.asarray(v) for k, v in inputs.items()}
    x = a["x"].reshape(B, C, N)
    split = lambda v: np.tile(v, 2)
    head = lambda v: np.repeat(v.reshape(HEADS, 1, HD), B, 1).reshape(P)
    par = np.zeros((P, NPAR), np.float32)
    for col, kind in ((GAMMA, "g"), (BETA, "b"), (MEAN, "m"), (VAR, "v")):
        qk = a[f"conv_{kind}_qk"]
        par[:, col] = split(qk[:C])
        par[:, col + 1] = split(qk[C:])
        par[:, col + 2] = head(a[f"conv_{kind}_v"])
        par[:, col + 3] = split(a[f"conv_{kind}_p"])
    par[:, LNG:LNG + E] = np.tile(a["ffn_ln_g"].T, (2, 1))
    par[:C, LNB:LNB + E] = a["ffn_ln_b"].T
    par[:, B2:B2 + EP] = a["ffn_b2"].reshape(EP, P).T
    par[:, B1:B1 + CH] = a["ffn_b1"].reshape(CH, P).T
    par[:, BR:BR + E] = a["ffn_br"]
    par[:C, WR:WR + E] = a["ffn_Wr"]
    wqkv = np.zeros((B, C, 3, P), np.float32)
    wproj = np.zeros((HEADS, B, HD, B, 2, C), np.float32)
    wv = np.zeros((B, C, HEADS, B, HD), np.float32)
    for b in range(B):
        wqkv[b, :, 0, b * C:(b + 1) * C] = a["conv_w_qk"][:C].T
        wqkv[b, :, 1, b * C:(b + 1) * C] = a["conv_w_qk"][C:].T
        wv[b, :, :, b, :] = a["conv_w_v"].T.reshape(C, HEADS, HD)
        for copy in range(2):
            wproj[:, b, :, b, copy, :] = a["conv_w_p"].T.reshape(HEADS, HD, C)
    wqkv[:, :, 2, :] = wv.reshape(B, C, P)
    arrays = {
        "x_split": x.reshape(P, N),
        "x_double": np.tile(x.transpose(1, 0, 2), (2, 1, 1)),
        "consts": shape_constants(),
        "params": par,
        "wqkv": wqkv.reshape(P, 3, P),
        "wproj": wproj.reshape(P, B, P),
        "w1": a["ffn_W1"].transpose(1, 0, 2).reshape(C, E * HID),
        "w2": a["ffn_W2"].reshape(CH, P, C).transpose(1, 0, 2),
    }
    arrays = {k: np.ascontiguousarray(v) for k, v in arrays.items()}
    nc = bacc.Bacc("TRN2", target_bir_lowering=False, num_devices=1)
    aps = [nc.dram_tensor(k, v.shape, F32, kind="ExternalInput").ap() for k, v in arrays.items()]
    out = nc.dram_tensor("out", (HALVES, C, B, NH), F32, kind="ExternalOutput").ap()
    metaformer(nc, *aps, out)
    r = run_bass_kernel_spmd(nc, [arrays], core_ids=[0])
    got = np.asarray(r.results[0]["out"])
    return np.ascontiguousarray(got.transpose(2, 1, 0, 3)).reshape(a["x"].shape)
```

```python
from contextlib import ExitStack

import numpy as np
import concourse.bass as bass
from concourse import mybir

F32 = mybir.dt.float32
F32R = mybir.dt.float32r
BF16 = mybir.dt.bfloat16
U32 = mybir.dt.uint32
ALU = mybir.AluOpType
ACT = mybir.ActivationFunctionType
AX = mybir.AxisListType

P = 128
B, C, N = 2, 64, 256
HEADS, HD = 8, 8
AREAS = 4
T = N // AREAS
HALVES = 2
NH = N // HALVES
AH = AREAS // HALVES
HP = HEADS // 2
E, HID = 8, 256
CH = E * HID // P
CE = HID // P
EP = E // 2
EPS_BN, EPS_C, EPS_T = 1e-5, 1e-6, 1e-5

CENTER = N
MEAN_B = CENTER + P
IDENT = 0
MEAN_D = IDENT + P
HMASK = MEAN_D + 1
IOTA = HMASK + HEADS
NEGHALF = IOTA + E
QSCALE = NEGHALF + 4
FOLD = QSCALE + 8
NCONST = FOLD + C

GAMMA, BETA, MEAN, VAR = 0, 4, 8, 12
LNG = 16
LNB = LNG + E
B2 = LNB + E
B1 = B2 + EP
BR = B1 + CH
WR = BR + E
NPAR = WR + E

H_RING, G_RING = 3, 6
LAG = 2
NORM2_AT = 3
BIAS_EARLY = 6
FILL = [0, 0, 0, 0, 0, 0]
WARM = 6


def metaformer(nc, x_split, x_double, consts, params, wqkv, wproj, w1, w2, out):
    ctx = ExitStack()
    with ctx:
        def sb(name, shape, dt=F32):
            return ctx.enter_context(nc.sbuf_tensor(name, shape, dt))

        def sem(name):
            return ctx.enter_context(nc.semaphore(name))

        xs = sb("xs", [P, N + P + B])
        xd = sb("xd", [P, B, N])
        cst = sb("cst", [P, NCONST])
        par = sb("par", [P, NPAR])
        wq = sb("wq", [P, 3, P])
        wp = sb("wp", [P, B, P])
        w1s = sb("w1s", [P, E * HID])
        w2s = sb("w2s", [P, CH, C])
        warm = sb("warm", [P, 512], BF16)
        xc = sb("xc", [P, N])
        sq = sb("sq", [P, N])
        vare = sb("vare", [P, HALVES, B])
        rstd = sb("rstd", [P, HALVES, B])
        rstdw = sb("rstdw", [P, HALVES, B, C])
        xn = sb("xn", [P, N])
        kaff = sb("kaff", [P, N])
        kmask = sb("kmask", [P, AREAS, HEADS, T])
        qblk = sb("qblk", [P, AREAS, B, T])
        vblk = sb("vblk", [P, AREAS * HP, 32])
        bnv = sb("bnv", [P, 4])
        bnr = sb("bnr", [P, 4])
        bnst0 = sb("bnst0", [P, 8])
        bnms = sb("bnms", [P, 4])
        bnst = sb("bnst", [P, 8])
        ptot = sb("ptot", [P, 1])
        xt = sb("xt", [P, B, N])
        rowmax = sb("rowmax", [P, 2, HEADS])
        sdif = sb("sdif", [P, 2, HEADS, T])
        prob = sb("prob", [P, 2, HEADS * T])
        rsum = sb("rsum", [P, AREAS, HEADS])
        rz = sb("rz", [P, AREAS, HEADS])
        rzw = sb("rzw", [P, AREAS, HEADS, P // HEADS])
        probT = sb("probT", [P, 2, HP, P])
        rzs = sb("rzs", [P, HALVES, AH * P])
        on = sb("on", [P, HALVES, AH, B, T])
        x1 = sb("x1", [P, HALVES, B, NH])
        xc2 = sb("xc2", [P, HALVES, B, NH])
        sq2 = sb("sq2", [P, HALVES, B, NH])
        var2 = sb("var2", [P, HALVES, 2, B])
        rstd2 = sb("rstd2", [P, HALVES, 2, B])
        rstdw2 = sb("rstdw2", [P, HALVES, B, P])
        xn2 = sb("xn2", [P, HALVES, B * NH])
        xr = sb("xr", [P, HALVES, B * NH], F32R)
        lgs = sb("lgs", [P, HALVES, B, E])
        lg = sb("lg", [P, HALVES, B, E])
        top = sb("top", [P, HALVES, B, 8])
        topi = sb("topi", [P, HALVES, B, 8], U32)
        dif = sb("dif", [P, HALVES, B])
        th = sb("th", [P, HALVES, B])
        g12 = sb("g12", [P, HALVES, 2, B])
        eq = sb("eq", [P, HALVES, 2, B, E])
        gate = sb("gate", [P, B, E, C])
        gateT = sb("gateT", [P, HALVES, EP, B * NH])
        w1hi = sb("w1hi", [P, E * HID], F32R)
        w1lo = sb("w1lo", [P, E * HID], F32R)
        w1g = sb("w1g", [P, 2, HID])
        cb = sb("cb", [P, CH])
        hg = sb("hg", [P, G_RING, B * NH])
        yg = sb("yg", [P, 2, B * NH])
        acc = sb("acc", [P, HALVES, B * NH])
        res = sb("res", [C, HALVES, B, NH])
        tiny = sb("tiny", [P, 1])

        bank = [ctx.enter_context(nc.psum_tensor(f"bank{i}", [P, 512], F32)) for i in range(8)]
        XC = [bank[7], bank[6]]
        VARB = [bank[5], bank[4]]
        RB = [bank[3], bank[2]]
        QP = [bank[0], bank[4]]
        KP = [bank[1], bank[5]]
        VP = [bank[7], bank[6]]
        S = [bank[0], bank[1]]
        BIAS = bank[7][:, 400:400 + CH]
        PT = [bank[2], bank[3]]
        OT = [bank[4], bank[5]]
        RZ = bank[6]
        MISC = bank[7]
        ROUT = [bank[4], bank[5]]
        GATE = [bank[4], bank[5]]
        H = [bank[0], bank[1], bank[2]]
        Y = [bank[3], bank[6]]
        FIN = [bank[4], bank[5]]

        ident = cst[:, IDENT:IDENT + P]

        (l_xs, l_cst, l_par, l_wq, l_wp, l_xd, l_w1a, l_w1b, l_w2) = (
            sem("l_" + n) for n in ("xs", "cst", "par", "wq", "wp", "xd", "w1a", "w1b", "w2"))
        stored = sem("stored")
        (p_xc, p_var, p_rb, p_q, p_k, p_v, p_pt, p_s, p_t, p_o, p_rz, p_cb, p_proj, p_xc2, p_var2,
         p_rb2, p_lg, p_gate, p_h, p_y, p_fin) = (sem("p_" + n) for n in (
            "xc", "var", "rb", "q", "k", "v", "ptot", "s", "t", "o", "rz", "cb", "proj", "xc2",
            "var2", "rb2", "lg", "gate", "h", "y", "fin"))
        (a_sq, a_q, a_v, a_p, a_pt, a_rzs, a_sq2, a_th, a_g) = (sem("a_" + n) for n in (
            "sq", "q", "v", "prob", "probT", "rzs", "sq2", "tanh", "gelu"))
        (v_xc, v_vare, v_xn, v_bn, v_kaff, v_kmask, v_ptot, v_xt, v_max, v_sub, v_sum, v_rz, v_on,
         v_x1, v_xc2, v_var2, v_xn2, v_hi, v_lo, v_lg, v_top, v_g12, v_eq, v_gate, v_gateT,
         v_cb, v_yg, v_acc, v_res, v_rstdw, v_rzw, v_rstdw2) = (sem("v_" + n) for n in (
            "xc", "vare", "xn", "bn", "kaff", "kmask", "ptot", "xt", "max", "sub", "sum", "rz",
            "on", "x1", "xc2", "var2", "xn2", "hi", "lo", "lg", "top", "g12", "eq", "gate",
            "gateT", "cb", "yg", "acc", "res", "rstdw", "rzw", "rstdw2"))
        (g_warm, g_zero, g_rstd, g_bnr, g_kmask, g_w1hi, g_w1g, g_w1lo, g_rstd2) = (
            sem("g_" + n) for n in (
                "warm", "zero", "rstd", "bnr", "kmask", "w1hi", "w1g", "w1lo", "rstd2"))

        block = ctx.enter_context(nc.Block())

        @block.sync
        def _(sp):
            sp.dma_start(xs[:, :], x_split).then_inc(l_xs, 16)
            sp.dma_start(par[:, :], params).then_inc(l_par, 16)
            sp.dma_start(cst[:, :], consts).then_inc(l_cst, 16)
            sp.dma_start(w1s[0:C, :], w1).then_inc(l_w1a, 16)
            sp.dma_start(wq[:, :, :], wqkv).then_inc(l_wq, 16)
            sp.dma_start(w1s[C:P, :], w1).then_inc(l_w1b, 16)
            sp.dma_start(wp[:, :, :], wproj).then_inc(l_wp, 16)
            sp.dma_start(xd[:, :, :], x_double).then_inc(l_xd, 16)
            sp.dma_start(w2s[:, :, :], w2).then_inc(l_w2, 16)
            for f in range(HALVES):
                sp.wait_ge(v_res, f + 1)
                sp.dma_start(out[f], res[:, f]).then_inc(stored, 16)
            sp.wait_ge(stored, 16 * HALVES)

        @block.gpsimd
        def _(pool):
            pool.memset(warm[:, :], 0.0).then_inc(g_warm, 1)
            pool.memset(qblk[:, :, :, :], 0.0).then_inc(g_zero, 1)
            pool.memset(vblk[:, :, :], 0.0).then_inc(g_zero, 1)
            pool.wait_ge(l_cst, 16)
            pool.wait_ge(v_bn, 1)
            pool.tensor_tensor(bnr[:, :], bnv[:, :], cst[:, NEGHALF:NEGHALF + 4], ALU.pow)\
                .then_inc(g_bnr, 1)
            for f in range(HALVES):
                pool.wait_ge(v_vare, f + 1)
                pool.tensor_tensor(rstd[:, f], vare[:, f], cst[:, NEGHALF:NEGHALF + B], ALU.pow)\
                    .then_inc(g_rstd, 1)
            pool.wait_ge(l_par, 16)
            pool.wait_ge(l_w1a, 16)
            pool.wait_ge(l_w1b, 16)

            def w1_hi(e):
                cols = slice(e * HID, (e + 1) * HID)
                pool.tensor_scalar(w1hi[:, cols], w1s[:, cols], par[:, LNG + e:LNG + e + 1], 1.0,
                                   ALU.mult, ALU.mult).then_inc(g_w1hi, 1)

            def w1_g(e):
                if e >= 2:
                    pool.wait_ge(g_w1lo, e - 1)
                cols = slice(e * HID, (e + 1) * HID)
                pool.tensor_scalar(w1g[:, e % 2], w1s[:, cols], par[:, LNG + e:LNG + e + 1], 1.0,
                                   ALU.mult, ALU.mult).then_inc(g_w1g, 1)

            def w1_lo(e):
                cols = slice(e * HID, (e + 1) * HID)
                pool.wait_ge(g_w1g, e + 1)
                pool.wait_ge(g_w1hi, e + 1)
                pool.tensor_tensor(w1lo[:, cols], w1g[:, e % 2], w1hi[:, cols].bitcast(F32),
                                   ALU.subtract).then_inc(g_w1lo, 1)

            def norm2(f):
                for i in range(2):
                    pool.wait_ge(v_var2, 2 * f + i + 1)
                    pool.tensor_tensor(rstd2[:, f, i], var2[:, f, i],
                                       cst[:, NEGHALF:NEGHALF + B], ALU.pow).then_inc(g_rstd2, 1)

            for a in range(1, AREAS, 2):
                pool.wait_ge(v_kaff, a // AH + 1)
                pool.tensor_tensor(
                    kmask[:, a], kaff[:, None, a * T:(a + 1) * T].broadcast_to((P, HEADS, T)),
                    cst[:, HMASK:HMASK + HEADS, None].broadcast_to((P, HEADS, T)), ALU.mult)\
                    .then_inc(g_kmask, 1)
            for e in range(E):
                w1_hi(e)
                w1_g(e)
                w1_lo(e)
                if e == NORM2_AT:
                    norm2(0)
            norm2(1)

        @block.scalar
        def _(act):
            act.wait_ge(g_warm, 1)
            act.activation(tiny[:, :], warm[:, 0:1], ACT.Exp)
            act.wait_ge(p_xc, 1)
            act.activation(sq[:, 0:NH], XC[0][:, 0:NH], ACT.Square).then_inc(a_sq, 1)
            act.wait_ge(v_xc, 1)
            act.activation(sq[:, NH:N], XC[1][:, 0:NH], ACT.Square).then_inc(a_sq, 1)
            act.wait_ge(v_bn, 5)
            act.wait_ge(g_zero, 2)
            for f in range(HALVES):
                act.wait_ge(p_q, f + 1)
                for b in range(B):
                    rows = slice(b * C, (b + 1) * C)
                    act.activation(qblk[rows, AH * f:AH * (f + 1), b, :],
                                   QP[f][rows, 0:NH].rearrange("p (a i) -> p a i", a=AH),
                                   ACT.Identity, bias=bnst[rows, 4:5], scale=bnst[rows, 0:1])\
                        .then_inc(a_q, 1)
                act.wait_ge(p_v, f + 1)
                for i in range(AH):
                    for h in range(2):
                        rows, cols = slice(h * T, (h + 1) * T), slice(16 * h, 16 * h + 16)
                        a = AH * f + i
                        act.activation(vblk[rows, HP * a:HP * (a + 1), cols],
                                       VP[f][i * T:(i + 1) * T, 0:P].rearrange("p (a c) -> p a c", c=32)[:, :, cols],
                                       ACT.Copy).then_inc(a_v, 1)

            def exp(a):
                act.wait_ge(v_sub, a + 1)
                if a >= 2:
                    act.wait_ge(p_t, a - 1)
                    act.wait_ge(v_sum, a - 1)
                act.activation(prob[:, a % 2, :], sdif[:, a % 2].rearrange("p h j -> p (h j)"),
                               ACT.Exp).then_inc(a_p, 1)

            def turned(a):
                act.wait_ge(p_t, a + 1)
                if a >= 2:
                    act.wait_ge(p_o, a - 1)
                act.activation(probT[:, a % 2].rearrange("p h i -> p (h i)"), PT[a % 2][:, :],
                               ACT.Copy).then_inc(a_pt, 1)

            def inverse_sums(f):
                act.wait_ge(p_rz, f + 1)
                act.activation(rzs[:, f, :], RZ[:, f * AH * P:(f + 1) * AH * P], ACT.Copy,
                               scale=bnst[:, 2:3]).then_inc(a_rzs, 1)

            def squares2(f):
                act.wait_ge(p_xc2, f + 1)
                act.activation(sq2[:, f].rearrange("p b n -> p (b n)"), MISC[:, 0:B * NH],
                               ACT.Square).then_inc(a_sq2, 1)

            def tanh(f):
                act.wait_ge(v_top, 5 * f + 5)
                act.activation(th[:, f, :], dif[:, f, :], ACT.Tanh, scale=0.5).then_inc(a_th, 1)

            def gelu(f, c):
                n = f * CH + c
                if n == 0:
                    act.wait_ge(v_cb, 1)
                act.wait_ge(p_h, n + 1)
                if n >= G_RING:
                    act.wait_ge(p_y, n - G_RING + 1)
                act.activation(hg[:, n % G_RING, :], H[n % H_RING][:, 0:B * NH], ACT.Gelu,
                               bias=cb[:, c:c + 1]).then_inc(a_g, 1)

            exp(0)
            exp(1)
            turned(0)
            turned(1)
            inverse_sums(0)
            exp(2)
            squares2(0)
            exp(3)
            turned(2)
            turned(3)
            inverse_sums(1)
            act.activation(tiny[:, :], warm[:, 0:1], ACT.Gelu)
            pieces = {(0, 4): lambda: tanh(0), (0, 5): lambda: squares2(1), (0, 13): lambda: tanh(1)}
            for f in range(HALVES):
                for c in range(CH):
                    if (f, c) in pieces:
                        pieces[f, c]()
                    gelu(f, c)

        @block.vector
        def _(dve):
            dve.wait_ge(l_par, 16)
            dve.tensor_scalar(bnv[:, :], par[:, VAR:VAR + 4], EPS_BN, None, ALU.add).then_inc(v_bn, 1)
            dve.wait_ge(p_xc, 2)
            dve.tensor_copy(xc[:, NH:N], XC[1][:, 0:NH]).then_inc(v_xc, 1)
            dve.wait_ge(a_sq, 1)
            dve.tensor_copy(xc[:, 0:NH], XC[0][:, 0:NH]).then_inc(v_xc, 1)
            dve.wait_ge(g_bnr, 1)
            dve.tensor_tensor(bnst0[:, 0:4], par[:, GAMMA:GAMMA + 4], bnr[:, :], ALU.mult)\
                .then_inc(v_bn, 1)
            for f in range(HALVES):
                dve.wait_ge(p_var, f + 1)
                dve.tensor_scalar(vare[:, f, :], VARB[f][:, 0:B], EPS_C, None, ALU.add)\
                    .then_inc(v_vare, 1)
            dve.wait_ge(v_bn, 2)
            dve.tensor_tensor(bnms[:, :], par[:, MEAN:MEAN + 4], bnst0[:, 0:4], ALU.mult)\
                .then_inc(v_bn, 1)
            dve.wait_ge(v_bn, 3)
            dve.tensor_tensor(bnst0[:, 4:8], par[:, BETA:BETA + 4], bnms[:, :], ALU.subtract)\
                .then_inc(v_bn, 1)
            dve.wait_ge(v_bn, 4)
            dve.wait_ge(l_cst, 16)
            dve.tensor_tensor(bnst[:, :], bnst0[:, :], cst[:, QSCALE:QSCALE + 8], ALU.mult)\
                .then_inc(v_bn, 1)
            dve.wait_ge(v_xc, 2)
            for f in range(HALVES):
                dve.wait_ge(g_rstd, f + 1)
                dve.tensor_copy(rstdw[:, f], rstd[:, f, :, None].broadcast_to((P, B, C))).then_inc(v_rstdw, 1)
            for f in range(HALVES):
                dve.wait_ge(p_rb, f + 1)
                dve.tensor_tensor(xn[:, f * NH:(f + 1) * NH], xc[:, f * NH:(f + 1) * NH],
                                  RB[f][:, 0:NH], ALU.mult).then_inc(v_xn, 1)
            dve.wait_ge(v_bn, 5)

            def k_affine(f):
                dve.wait_ge(p_k, f + 1)
                dve.tensor_scalar(kaff[:, f * NH:(f + 1) * NH], KP[f][:, 0:NH], bnst[:, 1:2],
                                  bnst[:, 5:6], ALU.mult, ALU.add).then_inc(v_kaff, 1)

            def k_masked(a):
                dve.wait_ge(v_kaff, a // AH + 1)
                dve.tensor_tensor(
                    kmask[:, a], kaff[:, None, a * T:(a + 1) * T].broadcast_to((P, HEADS, T)),
                    cst[:, HMASK:HMASK + HEADS, None].broadcast_to((P, HEADS, T)), ALU.mult)\
                    .then_inc(v_kmask, 1)

            def score_max(a):
                dve.wait_ge(p_s, a + 1)
                dve.tensor_reduce(rowmax[:, a % 2, :], S[a % 2][:, :].rearrange("p (h j) -> p h j", h=HEADS),
                                  AX.X, ALU.max).then_inc(v_max, 1)

            def score_sub(a):
                dve.wait_ge(v_max, a + 1)
                if a >= 2:
                    dve.wait_ge(a_p, a - 1)
                dve.tensor_tensor(sdif[:, a % 2], S[a % 2][:, :].rearrange("p (h j) -> p h j", h=HEADS),
                                  rowmax[:, a % 2, :, None].broadcast_to((P, HEADS, T)),
                                  ALU.subtract).then_inc(v_sub, 1)

            def prob_sum(a):
                dve.wait_ge(a_p, a + 1)
                dve.tensor_reduce(rsum[:, a, :], prob[:, a % 2, :].rearrange("p (h j) -> p h j", h=HEADS),
                                  AX.X, ALU.add).then_inc(v_sum, 1)

            def prob_inverse(f):
                areas = slice(AH * f, AH * (f + 1))
                dve.wait_ge(v_sum, AH * (f + 1))
                dve.reciprocal(rz[:, areas, :], rsum[:, areas, :]).then_inc(v_rz, 1)
                dve.wait_ge(v_rz, f + 1)
                dve.tensor_copy(rzw[:, areas].rearrange("p a h r -> p (a h) r"),
                                rz[:, areas, :].rearrange("p a h -> p (a h)")[:, :, None]
                                .broadcast_to((P, AH * HEADS, P // HEADS))).then_inc(v_rzw, 1)

            def normalise(f):
                dve.wait_ge(p_o, AH * (f + 1))
                dve.wait_ge(a_rzs, f + 1)
                dve.tensor_tensor(on[:, f].rearrange("p a b i -> p (a b i)"), OT[f][:, 0:AH * P],
                                  rzs[:, f, :], ALU.mult).then_inc(v_on, 1)

            def residual(f):
                dve.wait_ge(p_proj, f + 1)
                dve.wait_ge(v_xt, 1)
                dve.scalar_tensor_tensor(out=x1[:, f], in0=MISC[:, 0:B * NH].rearrange("p (b n) -> p b n", b=B),
                                         scalar=bnst[:, 3:4], in1=xt[:, :, f * NH:(f + 1) * NH],
                                         op0=ALU.mult, op1=ALU.add).then_inc(v_x1, 1)

            def centred2(f):
                dve.wait_ge(a_sq2, f + 1)
                dve.tensor_copy(xc2[:, f].rearrange("p b n -> p (b n)"), MISC[:, 0:B * NH])\
                    .then_inc(v_xc2, 1)

            def variance2(f):
                dve.wait_ge(p_var2, f + 1)
                dve.tensor_scalar(var2[:, f, 0, :], ROUT[f][:, 0:B], 1.0 + EPS_T, EPS_T * EPS_T,
                                  ALU.mult, ALU.add).then_inc(v_var2, 1)
                dve.tensor_scalar(var2[:, f, 1, :], ROUT[f][:, 0:B], EPS_T, None, ALU.add)\
                    .then_inc(v_var2, 1)

            def spread2(f):
                dve.wait_ge(g_rstd2, 2 * f + 1)
                dve.tensor_copy(rstdw2[:, f], rstd2[:, f, 0, :, None].broadcast_to((P, B, P)))\
                    .then_inc(v_rstdw2, 1)

            def normed2(f):
                dve.wait_ge(p_rb2, f + 1)
                dve.wait_ge(v_xc2, f + 1)
                dve.tensor_tensor(xn2[:, f, :], xc2[:, f].rearrange("p b n -> p (b n)"),
                                  MISC[:, 0:B * NH], ALU.mult).then_inc(v_xn2, 1)
                dve.wait_ge(v_xn2, f + 1)
                dve.tensor_copy(xr[:, f, :], xn2[:, f, :]).then_inc(v_hi, 1)
                dve.wait_ge(v_hi, f + 1)
                dve.tensor_tensor(xr[C:P, f, :], xn2[C:P, f, :], xr[C:P, f, :].bitcast(F32),
                                  ALU.subtract).then_inc(v_lo, 1)

            def router(f):
                dve.wait_ge(p_lg, f + 1)
                dve.wait_ge(g_rstd2, 2 * f + 2)
                dve.tensor_tensor(lgs[:, f], ROUT[f][:, 64:64 + B * E].rearrange("p (b e) -> p b e", b=B),
                                  rstd2[:, f, 1, :, None].broadcast_to((P, B, E)), ALU.mult)\
                    .then_inc(v_lg, 1)
                dve.wait_ge(v_lg, 2 * f + 1)
                dve.tensor_tensor(lg[:, f], lgs[:, f], par[:, None, BR:BR + E].broadcast_to((P, B, E)),
                                  ALU.add).then_inc(v_lg, 1)
                dve.wait_ge(v_lg, 2 * f + 2)
                for b in range(B):
                    dve.max(top[:, f, b, :], lg[:, f, b, :]).then_inc(v_top, 1)
                dve.wait_ge(v_top, 5 * f + 2)
                for b in range(B):
                    dve.max_index(topi[:, f, b, :], top[:, f, b, :], lg[:, f, b, :]).then_inc(v_top, 1)
                dve.tensor_tensor(dif[:, f, :], top[:, f, :, 0], top[:, f, :, 1], ALU.subtract)\
                    .then_inc(v_top, 1)
                dve.wait_ge(v_top, 5 * f + 5)
                for i in range(2):
                    dve.tensor_tensor(eq[:, f, i], cst[:, None, IOTA:IOTA + E].broadcast_to((P, B, E)),
                                      topi[:, f, :, i:i + 1].broadcast_to((P, B, E)), ALU.is_equal)\
                        .then_inc(v_eq, 1)

            def gates(f):
                dve.wait_ge(a_th, f + 1)
                dve.tensor_scalar(g12[:, f, 0, :], th[:, f, :], 0.5, 0.5, ALU.mult, ALU.add)\
                    .then_inc(v_g12, 1)
                dve.tensor_scalar(g12[:, f, 1, :], th[:, f, :], -0.5, 0.5, ALU.mult, ALU.add)\
                    .then_inc(v_g12, 1)
                dve.wait_ge(v_g12, 2 * f + 2)
                for i in range(2):
                    dve.wait_ge(v_eq, 4 * f + 2)
                    dve.tensor_tensor(eq[:, f, i], eq[:, f, i],
                                      g12[:, f, i, :, None].broadcast_to((P, B, E)), ALU.mult)\
                        .then_inc(v_eq, 1)
                dve.wait_ge(v_eq, 4 * f + 4)
                if f == 1:
                    dve.wait_ge(p_gate, 2)
                dve.tensor_tensor(gate[:, :, :, :], eq[:, f, 0, :, :, None].broadcast_to((P, B, E, C)),
                                  eq[:, f, 1, :, :, None].broadcast_to((P, B, E, C)), ALU.add)\
                    .then_inc(v_gate, 1)

            def gates_turned(f, i):
                dve.wait_ge(p_gate, 2 * f + i + 1)
                dve.tensor_copy(gateT[:, f, 2 * i:2 * i + 2, :].rearrange("p e n -> p (e n)"),
                                GATE[f][:, :]).then_inc(v_gateT, 1)

            def mix(f, p):
                n = f * EP + p
                dve.wait_ge(p_y, f * CH + 2 * CE * (p + 1))
                dve.wait_ge(v_gateT, 2 * f + p // 2 + 1)
                dst = acc[:, f, :] if p == 0 else yg[:, p % 2, :]
                dve.scalar_tensor_tensor(out=dst, in0=Y[n % 2][:, 0:B * NH], scalar=par[:, B2 + p:B2 + p + 1],
                                         in1=gateT[:, f, p, :], op0=ALU.add, op1=ALU.mult)\
                    .then_inc(v_yg, 1)
                dve.wait_ge(v_yg, n + 1)
                if p > 0:
                    if p > 1:
                        dve.wait_ge(v_acc, f * (EP - 1) + p - 1)
                    dve.tensor_tensor(acc[:, f, :], acc[:, f, :], yg[:, p % 2, :], ALU.add)\
                        .then_inc(v_acc, 1)

            def result(f):
                dve.wait_ge(p_fin, f + 1)
                dve.tensor_tensor(res[:, f].rearrange("p b n -> p (b n)"), FIN[f][0:C, 0:B * NH],
                                  x1[0:C, f].rearrange("p b n -> p (b n)"), ALU.add).then_inc(v_res, 1)

            k_affine(0)
            k_masked(0)
            k_affine(1)
            k_masked(2)
            score_max(0)
            score_max(1)
            score_sub(0)
            score_sub(1)
            dve.wait_ge(p_pt, 1)
            dve.wait_ge(p_cb, 1)
            dve.tensor_tensor(cb[:, :], BIAS, par[:, B1:B1 + CH], ALU.add).then_inc(v_cb, 1)
            dve.tensor_scalar(ptot[:, :], MISC[:, 384:385], bnst[:, 3:4], bnst[:, 7:8], ALU.mult, ALU.add)\
                .then_inc(v_ptot, 1)
            prob_sum(0)
            prob_sum(1)
            prob_inverse(0)
            dve.wait_ge(l_xd, 16)
            dve.wait_ge(v_ptot, 1)
            dve.tensor_scalar(xt[:, :, :].rearrange("p b n -> p (b n)"), xd[:, :, :].rearrange("p b n -> p (b n)"),
                              ptot[:, 0:1], None, ALU.add).then_inc(v_xt, 1)
            score_max(2)
            score_max(3)
            score_sub(2)
            normalise(0)
            score_sub(3)
            residual(0)
            prob_sum(2)
            centred2(0)
            variance2(0)
            prob_sum(3)
            prob_inverse(1)
            spread2(0)
            normed2(0)
            normalise(1)
            router(0)
            residual(1)
            gates(0)
            gates_turned(0, 0)
            centred2(1)
            variance2(1)
            gates_turned(0, 1)
            mix(0, 0)
            spread2(1)
            normed2(1)
            mix(0, 1)
            router(1)
            mix(0, 2)
            gates(1)
            mix(0, 3)
            gates_turned(1, 0)
            gates_turned(1, 1)
            result(0)
            for p in range(EP):
                mix(1, p)
            result(1)

        @block.tensor
        def _(pe):
            def keep_warm(n, scratch):
                for _ in range(n):
                    pe.matmul(scratch[:, :], warm[:, 0:P], warm[:, :], start=True, stop=True)

            def expert_bias(c0, c1):
                if c0 == 0:
                    pe.wait_ge(l_w1a, 16)
                    pe.wait_ge(l_par, 16)
                    pe.wait_ge(v_xc, 2)
                    pe.wait_ge(a_sq, 2)
                elif c0 == BIAS_EARLY:
                    pe.wait_ge(a_v, 2 * AH)
                for c in range(c0, c1):
                    e = c // CE
                    mm = pe.matmul(BIAS[:, c:c + 1], w1s[0:C, c * P:(c + 1) * P],
                                   par[0:C, LNB + e:LNB + e + 1], start=True, stop=True)
                if c1 == CH:
                    mm.then_inc(p_cb, 1)

            pe.wait_ge(g_warm, 1)
            keep_warm(WARM, bank[0])
            pe.wait_ge(l_xs, 16)
            for f in range(HALVES):
                pe.matmul(XC[f][:, 0:NH], xs[:, CENTER:CENTER + P], xs[:, f * NH:(f + 1) * NH],
                          start=True, stop=True).then_inc(p_xc, 1)
            for f in range(HALVES):
                pe.wait_ge(a_sq, f + 1)
                pe.matmul(VARB[f][:, 0:B], sq[:, f * NH:(f + 1) * NH], xs[:, MEAN_B:MEAN_B + B],
                          start=True, stop=True).then_inc(p_var, 1)
            expert_bias(0, BIAS_EARLY)
            keep_warm(FILL[0], bank[0])
            pe.wait_ge(l_cst, 16)
            for f in range(HALVES):
                pe.wait_ge(v_rstdw, f + 1)
                pe.transpose(RB[f][:, 0:NH], rstdw[:, f].rearrange("p b c -> p (b c)"), ident)\
                    .then_inc(p_rb, 1)
            keep_warm(FILL[1], bank[0])
            pe.wait_ge(l_wq, 16)
            for f in range(HALVES):
                pe.wait_ge(v_xn, f + 1)
                x_f = xn[:, f * NH:(f + 1) * NH]
                if f == 1:
                    pe.wait_ge(v_vare, 2)
                pe.matmul(KP[f][:, 0:NH], wq[:, 1, :], x_f, start=True, stop=True).then_inc(p_k, 1)
                pe.matmul(QP[f][:, 0:NH], wq[:, 0, :], x_f, start=True, stop=True).then_inc(p_q, 1)
                if f == 0:
                    pe.wait_ge(v_xc, 2)
                    pe.wait_ge(a_sq, 2)
                mm = pe.matmul(VP[f][:, 0:P], x_f, wq[:, 2, :], start=True, stop=True)
                mm.then_inc(p_v, 1)

            def scores(a):
                if a < 2:
                    pe.wait_ge(a_q, 2 * B if a == 1 and AH == 1 else B)
                    pe.wait_ge(v_kaff, 1)
                if a >= 2:
                    pe.wait_ge(a_q, 2 * B)
                    pe.wait_ge(v_sub, a - 1)
                pe.wait_ge(g_kmask if a % 2 else v_kmask, a // 2 + 1)
                pe.matmul(S[a % 2][:, :], qblk[:, a].rearrange("p b i -> p (b i)"),
                          kmask[:, a].rearrange("p h j -> p (h j)"), start=True, stop=True)\
                    .then_inc(p_s, 1)

            def turn(a):
                pe.wait_ge(a_p, a + 1)
                if a < 2:
                    pe.wait_ge(v_xn, 2)
                else:
                    pe.wait_ge(a_pt, a - 1)
                for h in range(HP):
                    mm = pe.transpose(PT[a % 2][:, h * P:(h + 1) * P], prob[:, a % 2, h * P:(h + 1) * P], ident)
                mm.then_inc(p_t, 1)

            def attend(a):
                f, i = a // AH, a % AH
                pe.wait_ge(a_pt, a + 1)
                pe.wait_ge(a_v, 2 * AH * (f + 1))
                if a == 0:
                    pe.wait_ge(a_q, 2 * B)
                    pe.wait_ge(v_kaff, 2)
                for h in range(HP):
                    mm = pe.matmul(OT[f][32 * h:32 * h + 32, i * P:(i + 1) * P], vblk[:, a * HP + h, :],
                                   probT[:, a % 2, h, :], start=True, stop=True)
                mm.then_inc(p_o, 1)

            def inverse_rows(f):
                pe.wait_ge(v_rzw, f + 1)
                if f == 0:
                    pe.wait_ge(a_v, 2 * AH * HALVES)
                else:
                    pe.wait_ge(a_rzs, 1)
                for a in range(AH * f, AH * (f + 1)):
                    mm = pe.transpose(RZ[:, a * P:(a + 1) * P], rzw[:, a].rearrange("p h r -> p (h r)"), ident)
                mm.then_inc(p_rz, 1)

            def shift_of_v():
                pe.wait_ge(l_wp, 16)
                pe.wait_ge(v_bn, 5)
                pe.wait_ge(a_v, 2 * AH)
                pe.matmul(MISC[:, 384:385], wp[:, 0, :], bnst[:, 6:7], start=True, stop=True)\
                    .then_inc(p_pt, 1)

            def project(f):
                pe.wait_ge(v_on, f + 1)
                if f == 0:
                    pe.wait_ge(v_ptot, 1)
                    pe.wait_ge(v_cb, 1)
                else:
                    pe.wait_ge(v_xn2, 1)
                for b in range(B):
                    mm = pe.matmul(MISC[:, b * NH:(b + 1) * NH], wp[:, b, :], on[:, f, :, b, :],
                                   start=True, stop=True)
                mm.then_inc(p_proj, 1)

            def centre2(f):
                pe.wait_ge(v_x1, f + 1)
                pe.matmul(MISC[:, 0:B * NH], xs[:, CENTER:CENTER + P],
                          x1[:, f].rearrange("p b n -> p (b n)"), start=True, stop=True).then_inc(p_xc2, 1)

            def var2_rows(f):
                pe.wait_ge(a_sq2, f + 1)
                for b in range(B):
                    mm = pe.matmul(ROUT[f][:, b:b + 1], sq2[:, f, b, :], cst[:, MEAN_D:MEAN_D + 1],
                                   start=True, stop=True)
                mm.then_inc(p_var2, 1)

            def spread2(f):
                pe.wait_ge(v_rstdw2, f + 1)
                pe.wait_ge(v_xc2, f + 1)
                for b in range(B):
                    mm = pe.transpose(MISC[:, b * NH:(b + 1) * NH], rstdw2[:, f, b, :], ident)
                mm.then_inc(p_rb2, 1)

            def logits(f):
                pe.wait_ge(v_xc2, f + 1)
                pe.wait_ge(v_var2, 2 * f + 2)
                for b in range(B):
                    mm = pe.matmul(ROUT[f][:, 64 + b * E:64 + (b + 1) * E], xc2[:, f, b, :],
                                   par[:, WR:WR + E], start=True, stop=True)
                mm.then_inc(p_lg, 1)

            def gate_rows(f, i):
                if i == 0:
                    pe.wait_ge(v_gate, f + 1)
                else:
                    pe.wait_ge(v_gateT, 2 * f + 1)
                for p in range(2 * i, 2 * i + 2):
                    for b in range(B):
                        mm = pe.transpose(GATE[f][:, ((p % 2) * B + b) * NH:((p % 2) * B + b + 1) * NH],
                                          gate[:, b, 2 * p:2 * p + 2, :].rearrange("p e c -> p (e c)"), ident)
                mm.then_inc(p_gate, 1)

            def hidden(f, c):
                n = f * CH + c
                e = c // CE
                if f == 0 and c % CE == 0:
                    pe.wait_ge(g_w1hi, e + 1)
                    pe.wait_ge(g_w1lo, e + 1)
                if c == 0:
                    pe.wait_ge(v_lo, f + 1)
                if n >= H_RING:
                    pe.wait_ge(a_g, n - H_RING + 1)
                pe.matmul(H[n % H_RING][:, 0:B * NH], w1hi[:, c * P:(c + 1) * P], xr[:, f, :],
                          start=True, stop=False)
                pe.matmul(H[n % H_RING][:, 0:B * NH], w1lo[:, c * P:(c + 1) * P], xr[:, f, :],
                          start=False, stop=True).then_inc(p_h, 1)

            def expert_out(f, c):
                n = f * CH + c
                e, half = c // CE, c % CE
                pair = f * EP + e // 2
                if n == 0:
                    pe.wait_ge(l_w2, 16)
                if c % (2 * CE) == 0 and pair >= 2:
                    pe.wait_ge(v_yg, pair - 1)
                if n == 2 * CE:
                    pe.wait_ge(a_rzs, 2)
                pe.wait_ge(a_g, n + 1)
                rows = slice(C * (e % 2), C * (e % 2) + C)
                pe.matmul(Y[pair % 2][rows, 0:B * NH], w2s[:, c, :], hg[:, n % G_RING, :],
                          start=(half == 0), stop=(half == CE - 1)).then_inc(p_y, 1)

            def sum_rows(f):
                pe.wait_ge(v_acc, (EP - 1) * (f + 1))
                pe.wait_ge(v_gateT, 2 * f + 2)
                pe.matmul(FIN[f][0:C, 0:B * NH], cst[:, FOLD:FOLD + C], acc[:, f, :], start=True, stop=True)\
                    .then_inc(p_fin, 1)

            scores(0)
            scores(1)
            expert_bias(BIAS_EARLY, CH)
            shift_of_v()
            keep_warm(FILL[2], bank[3])
            scores(2)
            turn(0)
            turn(1)
            scores(3)
            attend(0)
            attend(1)
            inverse_rows(0)
            keep_warm(FILL[3], bank[5])
            project(0)
            keep_warm(FILL[4], bank[5])
            centre2(0)
            turn(2)
            var2_rows(0)
            turn(3)
            attend(2)
            logits(0)
            attend(3)
            keep_warm(FILL[5], bank[0])
            spread2(0)
            inverse_rows(1)
            between = {
                (0, 2): [lambda: project(1)],
                (0, 4): [lambda: centre2(1)],
                (0, 6): [lambda: var2_rows(1), lambda: gate_rows(0, 0)],
                (0, 7): [lambda: logits(1), lambda: gate_rows(0, 1)],
                (0, 9): [lambda: spread2(1)],
                (1, 1): [lambda: gate_rows(1, 0)],
                (1, 3): [lambda: gate_rows(1, 1)],
                (1, 4): [lambda: sum_rows(0)],
            }
            steps = [(f, c) for f in range(HALVES) for c in range(CH)]
            for n, (f, c) in enumerate(steps):
                hidden(f, c)
                if n >= LAG:
                    expert_out(*steps[n - LAG])
                for piece in between.get((f, c), []):
                    piece()
            for step in steps[-LAG:]:
                expert_out(*step)
            sum_rows(1)


def shape_constants():
    row = np.arange(P)
    same = row[:, None] // C == row[None, :] // C
    first = np.zeros((P, P + B), np.float32)
    first[:, 0:P] = np.eye(P) - same / C
    first[:, P:P + B] = (row[:, None] // C == np.arange(B)) / C
    c = np.zeros((P, NCONST), np.float32)
    c[:, IDENT:IDENT + P] = np.eye(P)
    c[:, MEAN_D] = 1.0 / P
    c[:, HMASK:HMASK + HEADS] = (row[:, None] % C) // HD == np.arange(HEADS)
    c[:, IOTA:IOTA + E] = np.arange(E)
    c[:, NEGHALF:NEGHALF + 4] = -0.5
    c[:, QSCALE:QSCALE + 8] = 1.0
    c[:, [QSCALE, QSCALE + 4]] = HD ** -0.5
    c[:, FOLD:FOLD + C] = row[:, None] % C == np.arange(C)
    return first, c


def kernel(**inputs):
    import concourse.bacc as bacc
    from concourse.bass_utils import run_bass_kernel_spmd

    a = {k.replace("L0_", ""): np.asarray(v) for k, v in inputs.items()}
    x = a["x"].reshape(B, C, N)
    split = lambda v: np.tile(v, 2)
    head = lambda v: np.repeat(v.reshape(HEADS, 1, HD), B, 1).reshape(P)
    par = np.zeros((P, NPAR), np.float32)
    for col, kind in ((GAMMA, "g"), (BETA, "b"), (MEAN, "m"), (VAR, "v")):
        qk = a[f"conv_{kind}_qk"]
        par[:, col] = split(qk[:C])
        par[:, col + 1] = split(qk[C:])
        par[:, col + 2] = head(a[f"conv_{kind}_v"])
        par[:, col + 3] = split(a[f"conv_{kind}_p"])
    par[:, LNG:LNG + E] = np.tile(a["ffn_ln_g"].T, (2, 1))
    par[:C, LNB:LNB + E] = a["ffn_ln_b"].T
    par[:, B2:B2 + EP] = a["ffn_b2"].reshape(EP, P).T
    par[:, B1:B1 + CH] = a["ffn_b1"].reshape(CH, P).T
    par[:, BR:BR + E] = a["ffn_br"]
    par[:C, WR:WR + E] = a["ffn_Wr"]
    wqkv = np.zeros((B, C, 3, P), np.float32)
    wproj = np.zeros((HEADS, B, HD, B, 2, C), np.float32)
    wv = np.zeros((B, C, HEADS, B, HD), np.float32)
    for b in range(B):
        wqkv[b, :, 0, b * C:(b + 1) * C] = a["conv_w_qk"][:C].T
        wqkv[b, :, 1, b * C:(b + 1) * C] = a["conv_w_qk"][C:].T
        wv[b, :, :, b, :] = a["conv_w_v"].T.reshape(C, HEADS, HD)
        for copy in range(2):
            wproj[:, b, :, b, copy, :] = a["conv_w_p"].T.reshape(HEADS, HD, C)
    wqkv[:, :, 2, :] = wv.reshape(B, C, P)
    first, rest = shape_constants()
    arrays = {
        "x_split": np.concatenate([x.reshape(P, N), first], 1),
        "x_double": np.tile(x.transpose(1, 0, 2), (2, 1, 1)),
        "consts": rest,
        "params": par,
        "wqkv": wqkv.reshape(P, 3, P),
        "wproj": wproj.reshape(P, B, P),
        "w1": a["ffn_W1"].transpose(1, 0, 2).reshape(C, E * HID),
        "w2": a["ffn_W2"].reshape(CH, P, C).transpose(1, 0, 2),
    }
    arrays = {k: np.ascontiguousarray(v) for k, v in arrays.items()}
    nc = bacc.Bacc("TRN2", target_bir_lowering=False, num_devices=1)
    aps = [nc.dram_tensor(k, v.shape, F32, kind="ExternalInput").ap() for k, v in arrays.items()]
    out = nc.dram_tensor("out", (HALVES, C, B, NH), F32, kind="ExternalOutput").ap()
    metaformer(nc, *aps, out)
    r = run_bass_kernel_spmd(nc, [arrays], core_ids=[0])
    got = np.asarray(r.results[0]["out"])
    return np.ascontiguousarray(got.transpose(2, 1, 0, 3)).reshape(a["x"].shape)
```

```python
from contextlib import ExitStack

import numpy as np
import concourse.bass as bass
from concourse import mybir

F32 = mybir.dt.float32
F32R = mybir.dt.float32r
BF16 = mybir.dt.bfloat16
U32 = mybir.dt.uint32
ALU = mybir.AluOpType
ACT = mybir.ActivationFunctionType
AX = mybir.AxisListType

P = 128
B, C, N = 2, 64, 256
HEADS, HD = 8, 8
AREAS = 4
T = N // AREAS
HALVES = 2
NH = N // HALVES
AH = AREAS // HALVES
HP = HEADS // 2
E, HID = 8, 256
CH = E * HID // P
CE = HID // P
EP = E // 2
EPS_BN, EPS_C, EPS_T = 1e-5, 1e-6, 1e-5

CENTER = N
MEAN_B = CENTER + P
IDENT = 0
MEAN_D = IDENT + P
HMASK = MEAN_D + 1
IOTA = HMASK + HEADS
NEGHALF = IOTA + E
QSCALE = NEGHALF + 4
FOLD = QSCALE + 8
BMASK = FOLD + C
NCONST = BMASK + B

GAMMA, BETA, MEAN, VAR = 0, 4, 8, 12
LNG = 16
LNB = LNG + E
B2 = LNB + E
B1 = B2 + EP
BR = B1 + CH
WR = BR + E
NPAR = WR + E

STEPS = CH // 2
H_RING, G_RING = 3, 4
WARM = 6


def chunk(s, i):
    return (2 * (s // CE) + i) * CE + s % CE


def metaformer(nc, x_split, x_double, consts, params, wqkv, wproj, w1, w2, out):
    ctx = ExitStack()
    with ctx:
        def sb(name, shape, dt=F32):
            return ctx.enter_context(nc.sbuf_tensor(name, shape, dt))

        def sem(name):
            return ctx.enter_context(nc.semaphore(name))

        xs = sb("xs", [P, N + P + B])
        xd = sb("xd", [P, B, N])
        cst = sb("cst", [P, NCONST])
        par = sb("par", [P, NPAR])
        wq = sb("wq", [P, 3, P])
        wp = sb("wp", [C, P])
        cs = sb("cs", [C, 2, 2, C])
        wps = sb("wps", [P, B, 2, P])
        w1s = sb("w1s", [P, E * HID])
        w2s = sb("w2s", [P, CH, C])
        warm = sb("warm", [P, 512], BF16)
        xc = sb("xc", [P, N])
        sq = sb("sq", [P, N])
        vare = sb("vare", [P, HALVES, B])
        rstd = sb("rstd", [P, HALVES, B])
        rstdw = sb("rstdw", [P, HALVES, B, C])
        xn = sb("xn", [P, N])
        ks = sb("ks", [P, N])
        qs = sb("qs", [P, N])
        kr = sb("kr", [P, N])
        qr = sb("qr", [P, N])
        kaff = sb("kaff", [P, AREAS // 2, T])
        kmask = sb("kmask", [P, AREAS, HEADS, T])
        qblk = sb("qblk", [P, AREAS, B, T])
        vblk = sb("vblk", [P, AREAS * HP, 32])
        bnv = sb("bnv", [P, 4])
        bnr = sb("bnr", [P, 4])
        bnst0 = sb("bnst0", [P, 8])
        bnms = sb("bnms", [P, 4])
        bnst = sb("bnst", [P, 8])
        ptot = sb("ptot", [P, 1])
        xt = sb("xt", [P, B, N])
        rowmax = sb("rowmax", [P, 2, HEADS])
        sdif = sb("sdif", [P, 2, HEADS, T])
        prob = sb("prob", [P, 2, HEADS * T])
        rsum = sb("rsum", [P, AREAS, HEADS])
        rz = sb("rz", [P, AREAS, HEADS])
        rzw = sb("rzw", [P, AREAS, HEADS, P // HEADS])
        probT = sb("probT", [P, 2, HP, P])
        rzs = sb("rzs", [P, HALVES, AH * P])
        on = sb("on", [P, HALVES, AH, B, T])
        xc2 = sb("xc2", [P, HALVES, B, NH])
        sq2 = sb("sq2", [P, HALVES, B, NH])
        var2 = sb("var2", [P, HALVES, 2, B])
        rstd2 = sb("rstd2", [P, HALVES, 2, B])
        rstdw2 = sb("rstdw2", [P, HALVES, B, P])
        xn2 = sb("xn2", [P, HALVES, B * NH])
        xr = sb("xr", [P, HALVES, B * NH], F32R)
        lgs = sb("lgs", [P, HALVES, B, E])
        lg = sb("lg", [P, HALVES, B, E])
        top = sb("top", [P, HALVES, B, 8])
        topi = sb("topi", [P, HALVES, B, 8], U32)
        dif = sb("dif", [P, HALVES, B])
        th = sb("th", [P, HALVES, B])
        g12 = sb("g12", [P, HALVES, 2, B])
        eq = sb("eq", [P, HALVES, 2, B, E])
        gate = sb("gate", [P, HALVES, B, E, C])
        gateT = sb("gateT", [P, HALVES, EP, B * NH])
        w1hi = sb("w1hi", [P, E * HID], F32R)
        w1lo = sb("w1lo", [P, E * HID], F32R)
        w1g = sb("w1g", [P, 2, HID])
        cb = sb("cb", [P, CH])
        hg = sb("hg", [P, G_RING, 2, B * NH])
        yg = sb("yg", [P, HALVES, EP, B * NH])
        acc = sb("acc", [P, HALVES, 3, B * NH])
        res = sb("res", [P, HALVES, NH])
        tiny = sb("tiny", [P, 1])

        bank = [ctx.enter_context(nc.psum_tensor(f"bank{i}", [P, 512], F32)) for i in range(8)]
        XC = [bank[7], bank[6]]
        VARB = [bank[5], bank[4]]
        RB = [bank[3], bank[2]]
        QP = [bank[0], bank[4]]
        KP = [bank[1], bank[5]]
        VP = [bank[7], bank[6]]
        S = [bank[0], bank[1]]
        BIAS = bank[5][:, 0:CH]
        PT = [bank[2], bank[3]]
        OT = [bank[4], bank[5]]
        RZ = bank[6]
        MISC = bank[7]
        ROUT = [bank[4], bank[5]]
        GATE = [bank[4], bank[5]]
        H = [bank[0], bank[1], bank[2]]
        Y = [bank[3], bank[6]]
        FIN = [bank[4], bank[5]]

        ident = cst[:, IDENT:IDENT + P]

        (l_xs, l_cst, l_par, l_wq, l_wp, l_xd, l_w1a, l_w1b, l_w2) = (
            sem("l_" + n) for n in ("xs", "cst", "par", "wq", "wp", "xd", "w1a", "w1b", "w2"))
        stored = sem("stored")
        (p_xc, p_var, p_rb, p_q, p_k, p_v, p_pt, p_s, p_t, p_o, p_rz, p_cb, p_wps, p_xc2, p_var2,
         p_rb2, p_lg, p_gate, p_h, p_y, p_fin) = (sem("p_" + n) for n in (
            "xc", "var", "rb", "q", "k", "v", "ptot", "s", "t", "o", "rz", "cb", "wps", "xc2",
            "var2", "rb2", "lg", "gate", "h", "y", "fin"))
        (a_sq, a_ks, a_qs, a_kaff, a_q, a_v, a_wps, a_p, a_pt, a_rzs, a_sq2, a_th, a_g) = (sem("a_" + n) for n in (
            "sq", "ks", "qs", "kaff", "q", "v", "wps", "prob", "probT", "rzs", "sq2", "tanh", "gelu"))
        (v_xc, v_vare, v_xn, v_bn, v_kr, v_qr, v_kmask, v_ptot, v_max, v_sub, v_sum, v_rz, v_on, v_var2,
         v_xn2, v_hi, v_lo, v_lg, v_top, v_g12, v_eq, v_cb, v_yg, v_res) = (
            sem("v_" + n) for n in (
                "xc", "vare", "xn", "bn", "kr", "qr", "kmask", "ptot", "max", "sub", "sum", "rz", "on",
                "var2", "xn2", "hi", "lo", "lg", "top", "g12", "eq", "cb", "yg", "res"))
        (xc2_ready, xt_ready, cs_ready, rstdw2_ready, rstdw_ready, rzw_ready) = (
            sem(n) for n in (
                "xc2_ready", "xt_ready", "cs_ready", "rstdw2_ready", "rstdw_ready", "rzw_ready"))
        gate_spread = [sem(f"gate_spread{i}") for i in range(2)]
        pairs_added = [sem(f"pairs_added{f}") for f in range(HALVES)]
        gate_turned = [sem(f"gate_turned{i}") for i in range(2)]
        (g_warm, g_zero, g_rstd, g_bnr, g_kmask, g_w1hi, g_w1g, g_w1lo, g_rstd2) = (
            sem("g_" + n) for n in (
                "warm", "zero", "rstd", "bnr", "kmask", "w1hi", "w1g", "w1lo", "rstd2"))

        block = ctx.enter_context(nc.Block())

        @block.sync
        def _(sp):
            sp.dma_start(xs[:, :], x_split).then_inc(l_xs, 16)
            sp.dma_start(par[:, :], params).then_inc(l_par, 16)
            sp.dma_start(cst[:, :], consts).then_inc(l_cst, 16)
            sp.dma_start(wq[:, :, :], wqkv).then_inc(l_wq, 16)
            sp.dma_start(w1s[0:C, :], w1).then_inc(l_w1a, 16)
            sp.dma_start(w1s[C:P, :], w1).then_inc(l_w1b, 16)
            sp.dma_start(wp[:, :], wproj).then_inc(l_wp, 16)
            sp.dma_start(xd[:, :, :], x_double).then_inc(l_xd, 16)
            sp.dma_start(w2s[:, :, :], w2).then_inc(l_w2, 16)
            for f in range(HALVES):
                sp.wait_ge(v_res, f + 1)
                sp.dma_start(out[:, f * NH:(f + 1) * NH], res[:, f, :]).then_inc(stored, 16)
            sp.wait_ge(stored, 16 * HALVES)

        @block.gpsimd
        def _(pool):
            def zeros():
                pool.memset(warm[:, :], 0.0).then_inc(g_warm, 1)
                pool.memset(qblk[:, :, :, :], 0.0).then_inc(g_zero, 1)
                pool.memset(vblk[:, :, :], 0.0).then_inc(g_zero, 1)

            def bn_inverse():
                pool.wait_ge(l_cst, 16)
                pool.wait_ge(v_bn, 1)
                pool.tensor_tensor(bnr[:, :], bnv[:, :], cst[:, NEGHALF:NEGHALF + 4], ALU.pow)\
                    .then_inc(g_bnr, 1)

            def norm1(f):
                pool.wait_ge(v_vare, f + 1)
                pool.tensor_tensor(rstd[:, f], vare[:, f], cst[:, NEGHALF:NEGHALF + B], ALU.pow)\
                    .then_inc(g_rstd, 1)

            def w1_hi(e):
                if e == 0:
                    pool.wait_ge(l_par, 16)
                    pool.wait_ge(l_w1a, 16)
                    pool.wait_ge(l_w1b, 16)
                cols = slice(e * HID, (e + 1) * HID)
                pool.tensor_scalar(w1hi[:, cols], w1s[:, cols], par[:, LNG + e:LNG + e + 1], 1.0,
                                   ALU.mult, ALU.mult).then_inc(g_w1hi, 1)

            def w1_g(e):
                if e == 0:
                    pool.wait_ge(l_par, 16)
                    pool.wait_ge(l_w1a, 16)
                    pool.wait_ge(l_w1b, 16)
                if e >= 2:
                    pool.wait_ge(g_w1lo, e - 1)
                cols = slice(e * HID, (e + 1) * HID)
                pool.tensor_scalar(w1g[:, e % 2], w1s[:, cols], par[:, LNG + e:LNG + e + 1], 1.0,
                                   ALU.mult, ALU.mult).then_inc(g_w1g, 1)

            def w1_lo(e):
                cols = slice(e * HID, (e + 1) * HID)
                pool.wait_ge(g_w1g, e + 1)
                pool.wait_ge(g_w1hi, e + 1)
                pool.tensor_tensor(w1lo[:, cols], w1g[:, e % 2], w1hi[:, cols].bitcast(F32),
                                   ALU.subtract).then_inc(g_w1lo, 1)

            def norm2(f, i):
                pool.wait_ge(v_var2, 2 * f + i + 1)
                pool.tensor_tensor(rstd2[:, f, i], var2[:, f, i],
                                   cst[:, NEGHALF:NEGHALF + B], ALU.pow).then_inc(g_rstd2, 1)

            def k_masked(a):
                pool.wait_ge(a_kaff, a // 2 + 1)
                pool.tensor_tensor(
                    kmask[:, a], kaff[:, None, a // 2, :].broadcast_to((P, HEADS, T)),
                    cst[:, HMASK:HMASK + HEADS, None].broadcast_to((P, HEADS, T)), ALU.mult)\
                    .then_inc(g_kmask, 1)

            def added(f, i):
                pool.wait_ge(v_yg, f * EP + i + 2)
                if i > 0:
                    pool.wait_ge(pairs_added[f], i)
                pool.tensor_tensor(acc[:, f, i, :], acc[:, f, i - 1, :] if i else yg[:, f, 0, :], yg[:, f, i + 1, :],
                                  ALU.add).then_inc(pairs_added[f], 1)

            zeros()
            bn_inverse()
            norm1(0)
            norm1(1)
            w1_hi(0)
            k_masked(1)
            w1_hi(1)
            w1_hi(2)
            w1_g(0)
            w1_hi(3)
            w1_hi(4)
            w1_lo(0)
            w1_g(1)
            w1_hi(5)
            w1_g(2)
            w1_lo(1)
            k_masked(3)
            w1_g(3)
            norm2(0, 0)
            norm2(0, 1)
            w1_lo(2)
            w1_g(4)
            w1_lo(3)
            w1_g(5)
            w1_lo(4)
            w1_hi(6)
            w1_lo(5)
            w1_g(6)
            w1_hi(7)
            w1_g(7)
            w1_lo(6)
            w1_lo(7)
            norm2(1, 0)
            norm2(1, 1)
            added(0, 2)

        @block.scalar
        def _(act):
            def exp_table():
                act.wait_ge(g_warm, 1)
                act.activation(tiny[:, :], warm[:, 0:1], ACT.Exp)

            def squares1(f):
                act.wait_ge(p_xc, f + 1)
                if f == 1:
                    act.wait_ge(v_xc, 1)
                act.activation(sq[:, f * NH:(f + 1) * NH], XC[f][:, 0:NH], ACT.Square).then_inc(a_sq, 1)

            def k_out(f):
                act.wait_ge(p_k, f + 1)
                act.wait_ge(v_bn, 5)
                act.activation(ks[:, f * NH:(f + 1) * NH], KP[f][:, 0:NH], ACT.Copy, scale=bnst[:, 1:2])\
                    .then_inc(a_ks, 1)

            def q_out(f):
                act.wait_ge(p_q, f + 1)
                act.wait_ge(v_bn, 5)
                act.activation(qs[:, f * NH:(f + 1) * NH], QP[f][:, 0:NH], ACT.Copy, scale=bnst[:, 0:1])\
                    .then_inc(a_qs, 1)

            def k_shifted(a):
                act.wait_ge(v_kr, a // AH + 1)
                act.activation(kaff[:, a // 2, :], kr[:, a * T:(a + 1) * T], ACT.Identity, bias=bnst[:, 5:6])\
                    .then_inc(a_kaff, 1)

            def q_blocks(f):
                act.wait_ge(v_qr, f + 1)
                act.wait_ge(g_zero, 2)
                for b in range(B):
                    rows = slice(b * C, (b + 1) * C)
                    act.activation(qblk[rows, AH * f:AH * (f + 1), b, :],
                                   qr[rows, f * NH:(f + 1) * NH].rearrange("p (a i) -> p a i", a=AH),
                                   ACT.Identity, bias=bnst[rows, 4:5])\
                        .then_inc(a_q, 1)

            def v_blocks(f):
                act.wait_ge(p_v, f + 1)
                act.wait_ge(g_zero, 2)
                for i in range(AH):
                    for h in range(2):
                        rows, cols = slice(h * T, (h + 1) * T), slice(16 * h, 16 * h + 16)
                        a = AH * f + i
                        act.activation(vblk[rows, HP * a:HP * (a + 1), cols],
                                       VP[f][i * T:(i + 1) * T, 0:P].rearrange("p (a c) -> p a c", c=32)[:, :, cols],
                                       ACT.Copy).then_inc(a_v, 1)

            def exp(a):
                act.wait_ge(v_sub, a + 1)
                if a >= 2:
                    act.wait_ge(p_t, a - 1)
                    act.wait_ge(v_sum, a - 1)
                act.activation(prob[:, a % 2, :], sdif[:, a % 2].rearrange("p h j -> p (h j)"),
                               ACT.Exp).then_inc(a_p, 1)

            def turned(a):
                act.wait_ge(p_t, a + 1)
                if a >= 2:
                    act.wait_ge(p_o, a - 1)
                act.activation(probT[:, a % 2].rearrange("p h i -> p (h i)"), PT[a % 2][:, :],
                               ACT.Copy).then_inc(a_pt, 1)

            def inverse_sums(f):
                act.wait_ge(p_rz, f + 1)
                act.activation(rzs[:, f, :], RZ[:, f * AH * P:(f + 1) * AH * P], ACT.Copy,
                               scale=bnst[:, 2:3]).then_inc(a_rzs, 1)

            def scaled_wp():
                act.wait_ge(p_wps, 1)
                for b in range(B):
                    act.activation(wps[:, b].rearrange("p k o -> p (k o)"), MISC[:, 0:2 * P], ACT.Copy,
                                   scale=cst[:, BMASK + b:BMASK + b + 1]).then_inc(a_wps, 1)

            def squares2(f):
                act.wait_ge(p_xc2, f + 1)
                act.activation(sq2[:, f].rearrange("p b n -> p (b n)"), MISC[:, 0:B * NH],
                               ACT.Square).then_inc(a_sq2, 1)

            def tanh(f):
                act.wait_ge(v_top, 5 * f + 5)
                act.activation(th[:, f, :], dif[:, f, :], ACT.Tanh, scale=0.5).then_inc(a_th, 1)

            def gelu(f, s):
                n = f * STEPS + s
                if n == 0:
                    act.wait_ge(v_cb, 1)
                if n >= G_RING:
                    act.wait_ge(p_y, n - G_RING + 1)
                for i in range(2):
                    c = chunk(s, i)
                    act.wait_ge(p_h, n + 1)
                    act.activation(hg[:, n % G_RING, i, :], H[n % H_RING][:, i * B * NH:(i + 1) * B * NH],
                                   ACT.Gelu, bias=cb[:, c:c + 1]).then_inc(a_g, 1)

            def centred2(f):
                act.wait_ge(p_xc2, f + 1)
                act.activation(xc2[:, f].rearrange("p b n -> p (b n)"), MISC[:, 0:B * NH], ACT.Copy)\
                    .then_inc(xc2_ready, 1)

            def spread2(f):
                act.wait_ge(g_rstd2, 2 * f + 1)
                act.activation(rstdw2[:, f], rstd2[:, f, 0, :, None].broadcast_to((P, B, P)), ACT.Copy)\
                    .then_inc(rstdw2_ready, 1)

            def gelu_table():
                act.activation(tiny[:, :], warm[:, 0:1], ACT.Gelu)

            exp_table()
            squares1(0)
            squares1(1)
            k_out(0)
            q_out(0)
            k_out(1)
            k_shifted(1)
            q_blocks(0)
            v_blocks(0)
            q_out(1)
            k_shifted(3)
            scaled_wp()
            exp(0)
            exp(1)
            v_blocks(1)
            turned(0)
            turned(1)
            q_blocks(1)
            inverse_sums(0)
            squares2(0)
            centred2(0)
            exp(2)
            exp(3)
            gelu_table()
            turned(2)
            turned(3)
            gelu(0, 0)
            gelu(0, 1)
            tanh(0)
            inverse_sums(1)
            gelu(0, 2)
            gelu(0, 3)
            squares2(1)
            centred2(1)
            gelu(0, 4)
            spread2(1)
            gelu(0, 5)
            gelu(0, 6)
            gelu(0, 7)
            tanh(1)
            gelu(1, 0)
            gelu(1, 1)
            gelu(1, 2)
            gelu(1, 3)
            gelu(1, 4)
            gelu(1, 5)
            gelu(1, 6)
            gelu(1, 7)

        @block.vector
        def _(dve):
            def bn_variance():
                dve.wait_ge(l_par, 16)
                dve.tensor_scalar(bnv[:, :], par[:, VAR:VAR + 4], EPS_BN, None, ALU.add).then_inc(v_bn, 1)

            def bn_scale():
                dve.wait_ge(g_bnr, 1)
                dve.tensor_tensor(bnst0[:, 0:4], par[:, GAMMA:GAMMA + 4], bnr[:, :], ALU.mult)\
                    .then_inc(v_bn, 1)

            def bn_mean():
                dve.wait_ge(v_bn, 2)
                dve.tensor_tensor(bnms[:, :], par[:, MEAN:MEAN + 4], bnst0[:, 0:4], ALU.mult)\
                    .then_inc(v_bn, 1)

            def bn_shift():
                dve.wait_ge(v_bn, 3)
                dve.tensor_tensor(bnst0[:, 4:8], par[:, BETA:BETA + 4], bnms[:, :], ALU.subtract)\
                    .then_inc(v_bn, 1)

            def bn_softmax_scale():
                dve.wait_ge(v_bn, 4)
                dve.wait_ge(l_cst, 16)
                dve.tensor_tensor(bnst[:, :], bnst0[:, :], cst[:, QSCALE:QSCALE + 8], ALU.mult)\
                    .then_inc(v_bn, 1)

            def projection_scale():
                dve.wait_ge(v_bn, 5)
                for k, src in enumerate((xs[0:C, CENTER:CENTER + C], cst[0:C, FOLD:FOLD + C])):
                    dve.tensor_scalar(cs[:, k], src[:, None, :].broadcast_to((C, 2, C)), bnst[0:C, 3:4], None,
                                      ALU.mult).then_inc(cs_ready, 1)

            def centred1(f):
                dve.wait_ge(p_xc, f + 1)
                if f == 0:
                    dve.wait_ge(a_sq, 1)
                dve.tensor_copy(xc[:, f * NH:(f + 1) * NH], XC[f][:, 0:NH]).then_inc(v_xc, 1)

            def variance1(f):
                dve.wait_ge(p_var, f + 1)
                dve.tensor_scalar(vare[:, f, :], VARB[f][:, 0:B], EPS_C, None, ALU.add)\
                    .then_inc(v_vare, 1)

            def spread1(f):
                dve.wait_ge(g_rstd, f + 1)
                dve.tensor_copy(rstdw[:, f], rstd[:, f, :, None].broadcast_to((P, B, C))).then_inc(rstdw_ready, 1)

            def normed1(f):
                dve.wait_ge(p_rb, f + 1)
                dve.wait_ge(v_xc, 2)
                dve.tensor_tensor(xn[:, f * NH:(f + 1) * NH], xc[:, f * NH:(f + 1) * NH],
                                  RB[f][:, 0:NH], ALU.mult).then_inc(v_xn, 1)

            def k_scaled(f):
                dve.wait_ge(a_ks, f + 1)
                dve.wait_ge(p_rb, f + 1)
                dve.tensor_tensor(kr[:, f * NH:(f + 1) * NH], ks[:, f * NH:(f + 1) * NH], RB[f][:, 0:NH],
                                  ALU.mult).then_inc(v_kr, 1)

            def q_scaled(f):
                dve.wait_ge(a_qs, f + 1)
                dve.wait_ge(p_rb, f + 1)
                dve.tensor_tensor(qr[:, f * NH:(f + 1) * NH], qs[:, f * NH:(f + 1) * NH], RB[f][:, 0:NH],
                                  ALU.mult).then_inc(v_qr, 1)

            def k_masked(a):
                dve.wait_ge(v_kr, a // AH + 1)
                dve.scalar_tensor_tensor(
                    out=kmask[:, a], in0=kr[:, None, a * T:(a + 1) * T].broadcast_to((P, HEADS, T)),
                    scalar=bnst[:, 5:6], in1=cst[:, HMASK:HMASK + HEADS, None].broadcast_to((P, HEADS, T)),
                    op0=ALU.add, op1=ALU.mult).then_inc(v_kmask, 1)

            def score_max(a):
                dve.wait_ge(p_s, a + 1)
                dve.tensor_reduce(rowmax[:, a % 2, :], S[a % 2][:, :].rearrange("p (h j) -> p h j", h=HEADS),
                                  AX.X, ALU.max).then_inc(v_max, 1)

            def score_sub(a):
                dve.wait_ge(v_max, a + 1)
                if a >= 2:
                    dve.wait_ge(a_p, a - 1)
                dve.tensor_tensor(sdif[:, a % 2], S[a % 2][:, :].rearrange("p (h j) -> p h j", h=HEADS),
                                  rowmax[:, a % 2, :, None].broadcast_to((P, HEADS, T)),
                                  ALU.subtract).then_inc(v_sub, 1)

            def prob_sum(a):
                dve.wait_ge(a_p, a + 1)
                dve.tensor_reduce(rsum[:, a, :], prob[:, a % 2, :].rearrange("p (h j) -> p h j", h=HEADS),
                                  AX.X, ALU.add).then_inc(v_sum, 1)

            def prob_inverse(f):
                areas = slice(AH * f, AH * (f + 1))
                dve.wait_ge(v_sum, AH * (f + 1))
                dve.reciprocal(rz[:, areas, :], rsum[:, areas, :]).then_inc(v_rz, 1)

            def prob_spread(f):
                areas = slice(AH * f, AH * (f + 1))
                dve.wait_ge(v_rz, f + 1)
                dve.tensor_copy(rzw[:, areas].rearrange("p a h r -> p (a h) r"),
                                rz[:, areas, :].rearrange("p a h -> p (a h)")[:, :, None]
                                .broadcast_to((P, AH * HEADS, P // HEADS))).then_inc(rzw_ready, 1)

            def normalise(f):
                dve.wait_ge(p_o, AH * (f + 1))
                dve.wait_ge(a_rzs, f + 1)
                dve.tensor_tensor(on[:, f].rearrange("p a b i -> p (a b i)"), OT[f][:, 0:AH * P],
                                  rzs[:, f, :], ALU.mult).then_inc(v_on, 1)

            def variance2(f):
                dve.wait_ge(p_var2, f + 1)
                dve.tensor_scalar(var2[:, f, 0, :], ROUT[f][:, 0:B], 1.0 + EPS_T, EPS_T * EPS_T,
                                  ALU.mult, ALU.add).then_inc(v_var2, 1)
                dve.tensor_scalar(var2[:, f, 1, :], ROUT[f][:, 0:B], EPS_T, None, ALU.add)\
                    .then_inc(v_var2, 1)

            def spread2(f):
                dve.wait_ge(g_rstd2, 2 * f + 1)
                dve.tensor_copy(rstdw2[:, f], rstd2[:, f, 0, :, None].broadcast_to((P, B, P)))\
                    .then_inc(rstdw2_ready, 1)

            def normed2(f):
                dve.wait_ge(p_rb2, f + 1)
                dve.wait_ge(xc2_ready, f + 1)
                dve.tensor_tensor(xn2[:, f, :], xc2[:, f].rearrange("p b n -> p (b n)"),
                                  MISC[:, 0:B * NH], ALU.mult).then_inc(v_xn2, 1)

            def normed2_hi(f):
                dve.wait_ge(v_xn2, f + 1)
                dve.tensor_copy(xr[:, f, :], xn2[:, f, :]).then_inc(v_hi, 1)

            def normed2_lo(f):
                dve.wait_ge(v_hi, f + 1)
                dve.tensor_tensor(xr[C:P, f, :], xn2[C:P, f, :], xr[C:P, f, :].bitcast(F32),
                                  ALU.subtract).then_inc(v_lo, 1)

            def router1(f):
                dve.wait_ge(p_lg, f + 1)
                dve.wait_ge(g_rstd2, 2 * f + 2)
                dve.tensor_tensor(lgs[:, f], ROUT[f][:, 64:64 + B * E].rearrange("p (b e) -> p b e", b=B),
                                  rstd2[:, f, 1, :, None].broadcast_to((P, B, E)), ALU.mult)\
                    .then_inc(v_lg, 1)

            def router2(f):
                dve.wait_ge(v_lg, 2 * f + 1)
                dve.tensor_tensor(lg[:, f], lgs[:, f], par[:, None, BR:BR + E].broadcast_to((P, B, E)),
                                  ALU.add).then_inc(v_lg, 1)

            def router3(f):
                dve.wait_ge(v_lg, 2 * f + 2)
                for b in range(B):
                    dve.max(top[:, f, b, :], lg[:, f, b, :]).then_inc(v_top, 1)

            def router4(f):
                dve.wait_ge(v_top, 5 * f + 2)
                for b in range(B):
                    dve.max_index(topi[:, f, b, :], top[:, f, b, :], lg[:, f, b, :]).then_inc(v_top, 1)
                dve.tensor_tensor(dif[:, f, :], top[:, f, :, 0], top[:, f, :, 1], ALU.subtract)\
                    .then_inc(v_top, 1)

            def router5(f):
                dve.wait_ge(v_top, 5 * f + 5)
                for i in range(2):
                    dve.tensor_tensor(eq[:, f, i], cst[:, None, IOTA:IOTA + E].broadcast_to((P, B, E)),
                                      topi[:, f, :, i:i + 1].broadcast_to((P, B, E)), ALU.is_equal)\
                        .then_inc(v_eq, 1)

            def gates1(f):
                dve.wait_ge(a_th, f + 1)
                dve.tensor_scalar(g12[:, f, 0, :], th[:, f, :], 0.5, 0.5, ALU.mult, ALU.add)\
                    .then_inc(v_g12, 1)
                dve.tensor_scalar(g12[:, f, 1, :], th[:, f, :], -0.5, 0.5, ALU.mult, ALU.add)\
                    .then_inc(v_g12, 1)

            def gates2(f):
                dve.wait_ge(v_g12, 2 * f + 2)
                for i in range(2):
                    dve.wait_ge(v_eq, 4 * f + 2)
                    dve.tensor_tensor(eq[:, f, i], eq[:, f, i],
                                      g12[:, f, i, :, None].broadcast_to((P, B, E)), ALU.mult)\
                        .then_inc(v_eq, 1)

            def gates_spread(f, i):
                dve.wait_ge(v_eq, 4 * f + 4)
                experts = slice(i * E // 2, (i + 1) * E // 2)
                shape = (P, B, E // 2, C)
                dve.tensor_tensor(gate[:, f, :, experts, :],
                                  eq[:, f, 0, :, experts, None].broadcast_to(shape),
                                  eq[:, f, 1, :, experts, None].broadcast_to(shape), ALU.add)\
                    .then_inc(gate_spread[i], 1)

            def gates_turned(f, i):
                dve.wait_ge(p_gate, 2 * f + i + 1)
                dve.tensor_copy(gateT[:, f, 2 * i:2 * i + 2, :].rearrange("p e n -> p (e n)"),
                                GATE[f][:, :]).then_inc(gate_turned[i], 1)

            def mix(f, p):
                n = f * EP + p
                dve.wait_ge(p_y, f * STEPS + CE * (p + 1))
                dve.wait_ge(gate_turned[p // 2], f + 1)
                dve.scalar_tensor_tensor(out=yg[:, f, p, :], in0=Y[n % 2][:, 0:B * NH],
                                         scalar=par[:, B2 + p:B2 + p + 1],
                                         in1=gateT[:, f, p, :], op0=ALU.add, op1=ALU.mult)\
                    .then_inc(v_yg, 1)

            def added(f, i):
                dve.wait_ge(v_yg, f * EP + i + 2)
                if i > 0:
                    dve.wait_ge(pairs_added[f], i)
                dve.tensor_tensor(acc[:, f, i, :], acc[:, f, i - 1, :] if i else yg[:, f, 0, :], yg[:, f, i + 1, :],
                                  ALU.add).then_inc(pairs_added[f], 1)

            def result(f):
                dve.wait_ge(p_fin, 1 + 2 * f)
                dve.scalar_tensor_tensor(out=res[:, f, :], in0=FIN[f][:, 0:NH], scalar=ptot[:, 0:1],
                                         in1=xs[:, f * NH:(f + 1) * NH], op0=ALU.add, op1=ALU.add)\
                    .then_inc(v_res, 1)

            def bias_sum():
                dve.wait_ge(p_cb, 1)
                dve.tensor_tensor(cb[:, :], BIAS, par[:, B1:B1 + CH], ALU.add).then_inc(v_cb, 1)

            def projected_shift():
                dve.wait_ge(p_pt, 1)
                dve.tensor_scalar(ptot[:, :], MISC[:, 384:385], bnst[:, 7:8], None, ALU.add)\
                    .then_inc(v_ptot, 1)

            def shifted_residual():
                dve.wait_ge(l_xd, 16)
                dve.wait_ge(v_ptot, 1)
                dve.tensor_scalar(xt[:, :, :].rearrange("p b n -> p (b n)"), xd[:, :, :].rearrange("p b n -> p (b n)"),
                                  ptot[:, 0:1], None, ALU.add).then_inc(xt_ready, 1)

            bn_variance()
            centred1(1)
            bn_scale()
            variance1(0)
            centred1(0)
            bn_mean()
            bn_shift()
            bn_softmax_scale()
            variance1(1)
            spread1(0)
            spread1(1)
            normed1(0)
            k_scaled(0)
            q_scaled(0)
            k_masked(0)
            normed1(1)
            k_scaled(1)
            q_scaled(1)
            projection_scale()
            score_max(0)
            score_max(1)
            score_sub(0)
            score_sub(1)
            projected_shift()
            prob_sum(0)
            prob_sum(1)
            shifted_residual()
            prob_inverse(0)
            prob_spread(0)
            k_masked(2)
            normalise(0)
            score_max(2)
            score_sub(2)
            score_max(3)
            variance2(0)
            score_sub(3)
            spread2(0)
            prob_sum(2)
            router1(0)
            normed2(0)
            normed2_hi(0)
            router2(0)
            normed2_lo(0)
            router3(0)
            prob_sum(3)
            bias_sum()
            router4(0)
            prob_inverse(1)
            prob_spread(1)
            gates1(0)
            router5(0)
            normalise(1)
            gates2(0)
            gates_spread(0, 0)
            gates_spread(0, 1)
            variance2(1)
            gates_turned(0, 0)
            router1(1)
            mix(0, 0)
            router2(1)
            normed2(1)
            router3(1)
            normed2_hi(1)
            gates_turned(0, 1)
            router4(1)
            normed2_lo(1)
            router5(1)
            gates1(1)
            mix(0, 1)
            gates2(1)
            gates_spread(1, 0)
            mix(0, 2)
            gates_spread(1, 1)
            added(0, 0)
            mix(0, 3)
            added(0, 1)
            gates_turned(1, 0)
            gates_turned(1, 1)
            mix(1, 0)
            mix(1, 1)
            added(1, 0)
            mix(1, 2)
            added(1, 1)
            mix(1, 3)
            result(0)
            result(1)

        @block.tensor
        def _(pe):
            def expert_bias(c):
                if c == 0:
                    pe.wait_ge(l_w1a, 16)
                    pe.wait_ge(l_par, 16)
                    pe.wait_ge(a_ks, 2)
                e = c // CE
                mm = pe.matmul(BIAS[:, c:c + 1], w1s[0:C, c * P:(c + 1) * P],
                               par[0:C, LNB + e:LNB + e + 1], start=True, stop=True)
                if c == CH - 1:
                    mm.then_inc(p_cb, 1)

            def fill(scratch):
                pe.matmul(scratch[:, :], warm[:, 0:P], warm[:, :], start=True, stop=True)

            def warm_up():
                pe.wait_ge(g_warm, 1)
                for _ in range(WARM):
                    fill(bank[0])

            def fill_later():
                pe.wait_ge(v_kr, 1)
                pe.wait_ge(v_qr, 1)
                pe.wait_ge(v_xn, 1)
                fill(bank[3])

            def centre1(f):
                pe.wait_ge(l_xs, 16)
                pe.matmul(XC[f][:, 0:NH], xs[:, CENTER:CENTER + P], xs[:, f * NH:(f + 1) * NH],
                          start=True, stop=True).then_inc(p_xc, 1)

            def var1_rows(f):
                pe.wait_ge(a_sq, f + 1)
                pe.matmul(VARB[f][:, 0:B], sq[:, f * NH:(f + 1) * NH], xs[:, MEAN_B:MEAN_B + B],
                          start=True, stop=True).then_inc(p_var, 1)

            def spread1(f):
                pe.wait_ge(l_cst, 16)
                pe.wait_ge(rstdw_ready, f + 1)
                pe.transpose(RB[f][:, 0:NH], rstdw[:, f].rearrange("p b c -> p (b c)"), ident)\
                    .then_inc(p_rb, 1)

            def project_k(f):
                pe.wait_ge(l_wq, 16)
                pe.wait_ge(v_xc, 2)
                if f == 1:
                    pe.wait_ge(v_vare, 1)
                pe.matmul(KP[f][:, 0:NH], wq[:, 1, :], xc[:, f * NH:(f + 1) * NH], start=True, stop=True)\
                    .then_inc(p_k, 1)

            def project_q(f):
                pe.wait_ge(l_wq, 16)
                pe.wait_ge(v_xc, 2)
                if f == 1:
                    pe.wait_ge(v_vare, 2)
                pe.matmul(QP[f][:, 0:NH], wq[:, 0, :], xc[:, f * NH:(f + 1) * NH], start=True, stop=True)\
                    .then_inc(p_q, 1)

            def project_v(f):
                pe.wait_ge(l_wq, 16)
                pe.wait_ge(v_xn, f + 1)
                pe.wait_ge(v_xc, 2)
                pe.wait_ge(a_sq, 2)
                pe.matmul(VP[f][:, 0:P], xn[:, f * NH:(f + 1) * NH], wq[:, 2, :], start=True, stop=True)\
                    .then_inc(p_v, 1)

            def scores(a):
                if a < 2:
                    pe.wait_ge(a_q, B)
                if a >= 2:
                    pe.wait_ge(a_q, 2 * B)
                    pe.wait_ge(v_sub, a - 1)
                pe.wait_ge(g_kmask if a % 2 else v_kmask, a // 2 + 1)
                pe.matmul(S[a % 2][:, :], qblk[:, a].rearrange("p b i -> p (b i)"),
                          kmask[:, a].rearrange("p h j -> p (h j)"), start=True, stop=True)\
                    .then_inc(p_s, 1)

            def turn(a):
                pe.wait_ge(a_p, a + 1)
                if a < 2:
                    pe.wait_ge(v_xn, 2)
                    pe.wait_ge(v_kr, 2)
                    pe.wait_ge(v_qr, 2)
                else:
                    pe.wait_ge(a_pt, a - 1)
                for h in range(HP):
                    mm = pe.transpose(PT[a % 2][:, h * P:(h + 1) * P], prob[:, a % 2, h * P:(h + 1) * P], ident)
                mm.then_inc(p_t, 1)

            def attend(a):
                f, i = a // AH, a % AH
                pe.wait_ge(a_pt, a + 1)
                pe.wait_ge(a_v, 2 * AH * (f + 1))
                if a == 0:
                    pe.wait_ge(a_qs, 2)
                if a == AH:
                    pe.wait_ge(v_cb, 1)
                for h in range(HP):
                    mm = pe.matmul(OT[f][32 * h:32 * h + 32, i * P:(i + 1) * P], vblk[:, a * HP + h, :],
                                   probT[:, a % 2, h, :], start=True, stop=True)
                mm.then_inc(p_o, 1)

            def inverse_rows(f):
                pe.wait_ge(rzw_ready, f + 1)
                if f == 0:
                    pe.wait_ge(a_v, 2 * AH * HALVES)
                else:
                    pe.wait_ge(a_rzs, 1)
                for a in range(AH * f, AH * (f + 1)):
                    mm = pe.transpose(RZ[:, a * P:(a + 1) * P], rzw[:, a].rearrange("p h r -> p (h r)"), ident)
                mm.then_inc(p_rz, 1)

            def scale_wp():
                pe.wait_ge(l_wp, 16)
                pe.wait_ge(cs_ready, 2)
                pe.wait_ge(a_v, 2 * AH)
                pe.matmul(MISC[:, 0:2 * P], wp[:, :], cs[:, :, :, :].rearrange("p k t o -> p (k t o)"),
                          start=True, stop=True).then_inc(p_wps, 1)

            def shift_of_v():
                pe.wait_ge(v_bn, 5)
                pe.wait_ge(a_wps, 2)
                pe.matmul(MISC[:, 384:385], wps[:, 0, 1, :], bnst[:, 6:7], start=True, stop=True)\
                    .then_inc(p_pt, 1)

            def centre_residual(f):
                pe.wait_ge(xt_ready, 1)
                if f == 1:
                    pe.wait_ge(v_xn2, 1)
                pe.matmul(MISC[:, 0:B * NH], xs[:, CENTER:CENTER + P],
                          xt[:, :, f * NH:(f + 1) * NH], start=True, stop=False)

            def centre_projected(f):
                pe.wait_ge(a_wps, 2)
                pe.wait_ge(v_on, f + 1)
                for b in range(B):
                    mm = pe.matmul(MISC[:, b * NH:(b + 1) * NH], wps[:, b, 0, :], on[:, f, :, b, :],
                                   start=False, stop=(b == B - 1))
                mm.then_inc(p_xc2, 1)

            def var2_rows(f):
                pe.wait_ge(a_sq2, f + 1)
                for b in range(B):
                    mm = pe.matmul(ROUT[f][:, b:b + 1], sq2[:, f, b, :], cst[:, MEAN_D:MEAN_D + 1],
                                   start=True, stop=True)
                mm.then_inc(p_var2, 1)

            def spread2(f):
                pe.wait_ge(rstdw2_ready, f + 1)
                pe.wait_ge(xc2_ready, f + 1)
                for b in range(B):
                    mm = pe.transpose(MISC[:, b * NH:(b + 1) * NH], rstdw2[:, f, b, :], ident)
                mm.then_inc(p_rb2, 1)

            def logits(f):
                pe.wait_ge(xc2_ready, f + 1)
                pe.wait_ge(v_var2, 2 * f + 2)
                for b in range(B):
                    mm = pe.matmul(ROUT[f][:, 64 + b * E:64 + (b + 1) * E], xc2[:, f, b, :],
                                   par[:, WR:WR + E], start=True, stop=True)
                mm.then_inc(p_lg, 1)

            def gate_rows(f, i):
                pe.wait_ge(gate_spread[i], f + 1)
                if i == 1:
                    pe.wait_ge(gate_turned[0], f + 1)
                for p in range(2 * i, 2 * i + 2):
                    for b in range(B):
                        mm = pe.transpose(GATE[f][:, ((p % 2) * B + b) * NH:((p % 2) * B + b + 1) * NH],
                                          gate[:, f, b, 2 * p:2 * p + 2, :].rearrange("p e c -> p (e c)"), ident)
                mm.then_inc(p_gate, 1)

            def hidden(f, s):
                n = f * STEPS + s
                if f == 0 and s % CE == 0:
                    pe.wait_ge(g_w1hi, 2 * (s // CE) + 2)
                    pe.wait_ge(g_w1lo, 2 * (s // CE) + 2)
                if s == 0:
                    pe.wait_ge(v_lo, f + 1)
                if n >= H_RING:
                    pe.wait_ge(a_g, 2 * (n - H_RING + 1))
                for i in range(2):
                    dst = H[n % H_RING][:, i * B * NH:(i + 1) * B * NH]
                    cols = slice(chunk(s, i) * P, (chunk(s, i) + 1) * P)
                    pe.matmul(dst, w1hi[:, cols], xr[:, f, :], start=True, stop=False)
                    mm = pe.matmul(dst, w1lo[:, cols], xr[:, f, :], start=False, stop=True)
                mm.then_inc(p_h, 1)

            def expert_out(f, s):
                n = f * STEPS + s
                pair, half = f * EP + s // CE, s % CE
                if n == 0:
                    pe.wait_ge(l_w2, 16)
                if half == 0 and pair >= 2:
                    pe.wait_ge(v_yg, pair - 1)
                if n == CE:
                    pe.wait_ge(a_rzs, 2)
                pe.wait_ge(a_g, 2 * (n + 1))
                for i in range(2):
                    mm = pe.matmul(Y[pair % 2][i * C:(i + 1) * C, 0:B * NH], w2s[:, chunk(s, i), :],
                                   hg[:, n % G_RING, i, :], start=(half == 0), stop=(half == CE - 1))
                mm.then_inc(p_y, 1)

            def projected_rows(f):
                pe.wait_ge(gate_turned[1], f + 1)
                for b in range(B):
                    pe.matmul(FIN[f][b * C:(b + 1) * C, 0:NH], wps[:, b, 1, 0:C], on[:, f, :, b, :],
                              start=True, stop=False)

            def sum_rows(f, i):
                if f == 0:
                    pe.wait_ge(pairs_added[f], EP - 1)
                    pairs = acc[:, f, EP - 2, :]
                elif i == 0:
                    pe.wait_ge(pairs_added[f], EP - 2)
                    pairs = acc[:, f, EP - 3, :]
                else:
                    pe.wait_ge(v_yg, EP * (f + 1))
                    pairs = yg[:, f, EP - 1, :]
                for b in range(B):
                    mm = pe.matmul(FIN[f][b * C:(b + 1) * C, 0:NH], cst[:, FOLD:FOLD + C],
                                   pairs[:, b * NH:(b + 1) * NH], start=False, stop=(i == 1))
                mm.then_inc(p_fin, 1)

            warm_up()
            centre1(0)
            centre1(1)
            fill(bank[2])
            var1_rows(0)
            fill(bank[2])
            var1_rows(1)
            project_k(0)
            project_q(0)
            spread1(0)
            project_k(1)
            fill(bank[2])
            fill(bank[2])
            fill(bank[2])
            project_v(0)
            project_q(1)
            fill_later()
            spread1(1)
            scores(0)
            scores(1)
            scale_wp()
            for c in range(0, 2):
                expert_bias(c)
            fill_later()
            project_v(1)
            for c in range(2, 4):
                expert_bias(c)
            shift_of_v()
            for c in range(4, 5):
                expert_bias(c)
            fill_later()
            for c in range(5, 6):
                expert_bias(c)
            turn(0)
            turn(1)
            for c in range(6, 9):
                expert_bias(c)
            attend(0)
            attend(1)
            inverse_rows(0)
            centre_residual(0)
            scores(2)
            centre_projected(0)
            scores(3)
            var2_rows(0)
            for c in range(9, 15):
                expert_bias(c)
            logits(0)
            spread2(0)
            for c in range(15, CH):
                expert_bias(c)
            turn(2)
            turn(3)
            centre_residual(1)
            hidden(0, 0)
            hidden(0, 1)
            attend(2)
            attend(3)
            inverse_rows(1)
            hidden(0, 2)
            hidden(0, 3)
            expert_out(0, 0)
            hidden(0, 4)
            centre_projected(1)
            expert_out(0, 1)
            gate_rows(0, 0)
            var2_rows(1)
            expert_out(0, 2)
            hidden(0, 5)
            logits(1)
            gate_rows(0, 1)
            spread2(1)
            hidden(0, 6)
            hidden(0, 7)
            expert_out(0, 3)
            expert_out(0, 4)
            expert_out(0, 5)
            projected_rows(0)
            hidden(1, 0)
            hidden(1, 1)
            hidden(1, 2)
            expert_out(0, 6)
            expert_out(0, 7)
            hidden(1, 3)
            hidden(1, 4)
            gate_rows(1, 0)
            hidden(1, 5)
            expert_out(1, 0)
            expert_out(1, 1)
            gate_rows(1, 1)
            hidden(1, 6)
            hidden(1, 7)
            expert_out(1, 2)
            expert_out(1, 3)
            expert_out(1, 4)
            expert_out(1, 5)
            expert_out(1, 6)
            expert_out(1, 7)
            sum_rows(0, 1)
            projected_rows(1)
            sum_rows(1, 0)
            sum_rows(1, 1)
            fill_later()
            fill_later()
            fill_later()


def shape_constants():
    row = np.arange(P)
    same = row[:, None] // C == row[None, :] // C
    first = np.zeros((P, P + B), np.float32)
    first[:, 0:P] = np.eye(P) - same / C
    first[:, P:P + B] = (row[:, None] // C == np.arange(B)) / C
    c = np.zeros((P, NCONST), np.float32)
    c[:, IDENT:IDENT + P] = np.eye(P)
    c[:, MEAN_D] = 1.0 / P
    c[:, HMASK:HMASK + HEADS] = (row[:, None] % C) // HD == np.arange(HEADS)
    c[:, IOTA:IOTA + E] = np.arange(E)
    c[:, NEGHALF:NEGHALF + 4] = -0.5
    c[:, QSCALE:QSCALE + 8] = 1.0
    c[:, [QSCALE, QSCALE + 4]] = HD ** -0.5
    c[:, FOLD:FOLD + C] = row[:, None] % C == np.arange(C)
    c[:, BMASK:BMASK + B] = (row[:, None] // HD) % B == np.arange(B)
    return first, c


def kernel(**inputs):
    import concourse.bacc as bacc
    from concourse.bass_utils import run_bass_kernel_spmd

    a = {k.replace("L0_", ""): np.asarray(v) for k, v in inputs.items()}
    x = a["x"].reshape(B, C, N)
    split = lambda v: np.tile(v, 2)
    head = lambda v: np.repeat(v.reshape(HEADS, 1, HD), B, 1).reshape(P)
    par = np.zeros((P, NPAR), np.float32)
    for col, kind in ((GAMMA, "g"), (BETA, "b"), (MEAN, "m"), (VAR, "v")):
        qk = a[f"conv_{kind}_qk"]
        par[:, col] = split(qk[:C])
        par[:, col + 1] = split(qk[C:])
        par[:, col + 2] = head(a[f"conv_{kind}_v"])
        par[:, col + 3] = split(a[f"conv_{kind}_p"])
    par[:, LNG:LNG + E] = np.tile(a["ffn_ln_g"].T, (2, 1))
    par[:C, LNB:LNB + E] = a["ffn_ln_b"].T
    par[:, B2:B2 + EP] = a["ffn_b2"].reshape(EP, P).T
    par[:, B1:B1 + CH] = a["ffn_b1"].reshape(CH, P).T
    par[:, BR:BR + E] = a["ffn_br"]
    par[:C, WR:WR + E] = a["ffn_Wr"]
    wqkv = np.zeros((B, C, 3, P), np.float32)
    wv = np.zeros((B, C, HEADS, B, HD), np.float32)
    for b in range(B):
        wqkv[b, :, 0, b * C:(b + 1) * C] = a["conv_w_qk"][:C].T
        wqkv[b, :, 1, b * C:(b + 1) * C] = a["conv_w_qk"][C:].T
        wv[b, :, :, b, :] = a["conv_w_v"].T.reshape(C, HEADS, HD)
    wqkv[:, :, 2, :] = wv.reshape(B, C, P)
    first, rest = shape_constants()
    arrays = {
        "x_split": np.concatenate([x.reshape(P, N), first], 1),
        "x_double": np.tile(x.transpose(1, 0, 2), (2, 1, 1)),
        "consts": rest,
        "params": par,
        "wqkv": wqkv.reshape(P, 3, P),
        "wproj": np.repeat(a["conv_w_p"].reshape(C, HEADS, 1, HD), B, 2).reshape(C, P),
        "w1": a["ffn_W1"].transpose(1, 0, 2).reshape(C, E * HID),
        "w2": a["ffn_W2"].reshape(CH, P, C).transpose(1, 0, 2),
    }
    arrays = {k: np.ascontiguousarray(v) for k, v in arrays.items()}
    nc = bacc.Bacc("TRN2", target_bir_lowering=False, num_devices=1)
    aps = [nc.dram_tensor(k, v.shape, F32, kind="ExternalInput").ap() for k, v in arrays.items()]
    out = nc.dram_tensor("out", (P, N), F32, kind="ExternalOutput").ap()
    metaformer(nc, *aps, out)
    r = run_bass_kernel_spmd(nc, [arrays], core_ids=[0])
    got = np.asarray(r.results[0]["out"])
    return got.reshape(a["x"].shape)
```
